# Optimizing a Trainium2 kernel written in Bass

```python
import numpy as np
import jax
import jax.numpy as jnp

def _softmax(x, axis=-1):
    return jax.nn.softmax(x, axis=axis)

def _gelu(x):
    return jax.nn.gelu(x, approximate=True)

def _silu(x):
    return jax.nn.silu(x)

def _sigmoid(x):
    return jax.nn.sigmoid(x)

def _layernorm(x, axis=-1, eps=1e-05):
    m = jnp.mean(x, axis=axis, keepdims=True)
    v = jnp.var(x, axis=axis, keepdims=True)
    return (x - m) / jnp.sqrt(v + eps)

def _scatter_add(tgt, idx, src, axis=0):
    return tgt.at[idx].add(src)

def _segment_sum(src, seg, n):
    return jax.ops.segment_sum(src, seg, n)
kernel_name = 'mk_vit_tower_cls_d1_tok_img1024_r4_28602a'

def setup_inputs(seed: int=0):
    np.random.seed(seed)
    _w = jnp.asarray

    def _rec_inputs():
        import jax
        import jax.numpy as jnp
        _rk = jax.random.key(seed)
        x = -0.000125008 + 0.999885 * jax.random.normal(jax.random.fold_in(_rk, 1), (8, 512, 256, 4), jnp.float32)
        cls_tok = 0.02 * jax.random.normal(jax.random.fold_in(_rk, 5), (1, 1, 256), jnp.float32)
        return (x, cls_tok)
    x, cls_tok = _rec_inputs()

    def _L0_tok_setup():
        import jax, jax.numpy as jnp
        import numpy as np
        key = jax.random.key(seed)
        k1, k2, k3 = jax.random.split(key, 3)
        B, H, I, O, Dp1 = (4, 512, 256, 256, 4)
        x = jax.random.normal(k1, (B, H, I, Dp1), dtype=jnp.float32)
        weight = 0.1 * jax.random.normal(k2, (O, Dp1), dtype=jnp.float32)
        weighted_sum = 0.1 * jax.random.normal(k3, (O, I), dtype=jnp.float32)
        return {'x': x, 'weight': weight, 'weighted_sum': weighted_sum}
    _L0_tok_all = _L0_tok_setup()
    _L0_tok_in = {k: v for k, v in _L0_tok_all.items() if k in ('weight', 'weighted_sum')}
    del _L0_tok_all

    def _L0_attn_setup():
        import jax, jax.numpy as jnp
        import numpy as np
        D_MODEL = 256
        NUM_HEADS = 16
        D_K = D_MODEL // NUM_HEADS
        BATCH, SEQ = (2, 512)
        key = jax.random.key(seed)
        k = jax.random.split(key, 5)
        std = np.sqrt(2.0 / (D_MODEL + D_MODEL)).astype(np.float32)
        return {'x': jax.random.normal(k[0], (BATCH, SEQ, D_MODEL), dtype=jnp.float32), 'WQ': jax.random.normal(k[1], (D_MODEL, D_MODEL), dtype=jnp.float32) * std, 'WK': jax.random.normal(k[2], (D_MODEL, D_MODEL), dtype=jnp.float32) * std, 'WV': jax.random.normal(k[3], (D_MODEL, D_MODEL), dtype=jnp.float32) * std, 'WO': jax.random.normal(k[4], (D_MODEL, D_MODEL), dtype=jnp.float32) * std}
    _L0_attn_all = _L0_attn_setup()
    _L0_attn_in = {k: v for k, v in _L0_attn_all.items() if k in ('WQ', 'WK', 'WV', 'WO')}
    del _L0_attn_all

    def _L0_ffn_setup():
        import jax, jax.numpy as jnp
        import numpy as np
        B, S, H, R, F, E, K = (4, 512, 256, 64, 1024, 8, 2)
        key = jax.random.key(seed)
        k = jax.random.split(key, 7)
        s = 0.02
        return {'x': jax.random.normal(k[0], (B, S, H), dtype=jnp.float32), 'router_w': jax.random.normal(k[1], (H, E), dtype=jnp.float32) * s, 'router_b': jnp.zeros((E,), dtype=jnp.float32), 'w1': jax.random.normal(k[2], (E, H, R), dtype=jnp.float32) * s, 'w2': jax.random.normal(k[3], (E, R, F), dtype=jnp.float32) * s, 'lin2_w': jax.random.normal(k[4], (F, H), dtype=jnp.float32) * s, 'lin2_b': jnp.zeros((H,), dtype=jnp.float32)}
    _L0_ffn_all = _L0_ffn_setup()
    _L0_ffn_in = {k: v for k, v in _L0_ffn_all.items() if k in ('router_w', 'router_b', 'w1', 'w2', 'lin2_w', 'lin2_b')}
    del _L0_ffn_all
    return {'x': x, 'cls_tok': cls_tok, 'L0_tok_weight': _L0_tok_in['weight'], 'L0_tok_weighted_sum': _L0_tok_in['weighted_sum'], 'L0_attn_WQ': _L0_attn_in['WQ'], 'L0_attn_WK': _L0_attn_in['WK'], 'L0_attn_WV': _L0_attn_in['WV'], 'L0_attn_WO': _L0_attn_in['WO'], 'L0_ffn_router_w': _L0_ffn_in['router_w'], 'L0_ffn_router_b': _L0_ffn_in['router_b'], 'L0_ffn_w1': _L0_ffn_in['w1'], 'L0_ffn_w2': _L0_ffn_in['w2'], 'L0_ffn_lin2_w': _L0_ffn_in['lin2_w'], 'L0_ffn_lin2_b': _L0_ffn_in['lin2_b']}

def reference(x, cls_tok, L0_tok_weight, L0_tok_weighted_sum, L0_attn_WQ, L0_attn_WK, L0_attn_WV, L0_attn_WO, L0_ffn_router_w, L0_ffn_router_b, L0_ffn_w1, L0_ffn_w2, L0_ffn_lin2_w, L0_ffn_lin2_b):
    import jax
    import jax.numpy as jnp

    def _L0_tok_ref(x, weight, weighted_sum):
        import jax, jax.numpy as jnp
        import numpy as np
        return jnp.einsum('bhid,oi,od->bho', x, weighted_sum, weight)

    def _L0_attn_ref(x, WQ, WK, WV, WO):
        import jax, jax.numpy as jnp
        import numpy as np
        D_MODEL = 256
        NUM_HEADS = 16
        D_K = D_MODEL // NUM_HEADS
        BATCH, SEQ = (2, 512)
        B, S, E = x.shape
        mask = jnp.where(jnp.triu(jnp.ones((S, S), dtype=bool), k=1), -jnp.inf, 0.0).astype(x.dtype)

        def heads(W):
            return (x @ W).reshape(B, S, NUM_HEADS, D_K).transpose(0, 2, 1, 3)
        Q, K, V = (heads(WQ), heads(WK), heads(WV))
        score = jnp.einsum('bhqd,bhkd->bhqk', Q, K) / jnp.sqrt(jnp.asarray(D_K, x.dtype))
        score = score + mask
        score = score - jnp.max(score, axis=-1, keepdims=True)
        score = jnp.exp(score)
        score = score / jnp.sum(score, axis=-1, keepdims=True)
        out = jnp.einsum('bhqk,bhkd->bhqd', score, V)
        out = out.transpose(0, 2, 1, 3).reshape(B, S, E)
        return out @ WO

    def _L0_ffn_ref(x, router_w, router_b, w1, w2, lin2_w, lin2_b):
        import jax, jax.numpy as jnp
        import numpy as np
        B, S, H, R, F, E, K = (4, 512, 256, 64, 1024, 8, 2)
        logits = jnp.einsum('bsh,he->bse', x, router_w) + router_b
        routing_weights = jax.nn.softmax(logits, axis=-1)
        _, topk_idx = jax.lax.top_k(routing_weights, K)
        mask = jnp.sum(jax.nn.one_hot(topk_idx, E, dtype=x.dtype), axis=-2)
        mw = routing_weights * mask
        t = jnp.einsum('bsh,ehr->bser', x, w1)
        t = t * mw[..., None]
        mixed = jnp.einsum('bser,erf->bsf', t, w2)
        h = jax.nn.gelu(mixed, approximate=False)
        out = jnp.einsum('bsf,fh->bsh', h, lin2_w) + lin2_b
        return out
    h = _L0_tok_ref(x, L0_tok_weight, L0_tok_weighted_sum)
    h = jnp.concatenate([jnp.broadcast_to(cls_tok, (h.shape[0], 1, h.shape[2])), h], axis=1)
    h = h + _L0_attn_ref(_layernorm(h, axis=-1), L0_attn_WQ, L0_attn_WK, L0_attn_WV, L0_attn_WO)
    h = h + _L0_ffn_ref(_layernorm(h, axis=-1), L0_ffn_router_w, L0_ffn_router_b, L0_ffn_w1, L0_ffn_w2, L0_ffn_lin2_w, L0_ffn_lin2_b)
    return h

_drawn_inputs = setup_inputs


def setup_inputs(seed=0):
    import zlib

    import numpy as np

    out = dict(_drawn_inputs(seed))
    spreads = {'L0_ffn_router_b': (0.0, 0.8), 'L0_ffn_lin2_b': (0.0, 0.1)}
    factors = {'L0_ffn_router_w': 6.31, 'L0_ffn_w1': 5.38, 'L0_ffn_w2': 5.341, 'L0_ffn_lin2_w': 5.342}
    for name, (base, spread) in spreads.items():
        noise = np.random.default_rng([zlib.crc32(name.encode()), seed]).standard_normal(out[name].shape)
        drawn = base * np.exp(spread * noise) if base else spread * noise
        out[name] = jnp.asarray(drawn.astype(out[name].dtype))
    for name, factor in factors.items():
        out[name] = (out[name] * factor).astype(out[name].dtype)
    return out
```

```python
from contextlib import ExitStack

import concourse.bass as bass
from concourse import mybir

ALU = mybir.AluOpType
ACT = mybir.ActivationFunctionType
AX_X = mybir.AxisListType.X
F32 = mybir.dt.float32
BF16 = mybir.dt.bfloat16

P = 128
B, S, IN, DD = 8, 512, 256, 4
D, NH, DK = 256, 16, 16
NE, RK, F = 8, 64, 1024
NT = S // P
KX = IN * DD // P
HT = D // P
NC = NE * RK // P
NF = F // P
CHUNKS = 4 * NT
EPS = 1e-5
MASKED = -1e30
Q_PART = (0, 0, 1, 1, 0, 2)
K_PART = (0, 1, 0, 1, 2, 0)
STACK = DK * len(Q_PART)

MAX_UNITS = [(qt, h, n) for qt, n in ((0, 4), (1, 2), (2, 1), (3, 1)) for h in range(0, NH, n)]
EXP_UNITS = [[(j, 1) for j in range(4)], [(j, 1) for j in range(4)], [(0, 2), (2, 2)], [(0, 4)]]
N_EXP = 4 * sum(len(u) for u in EXP_UNITS)
S_CLS, S_MAX, S_MT, S_EXP = 0, 1, 1 + len(MAX_UNITS), 2 + len(MAX_UNITS)
S_USES = S_EXP + N_EXP
MAX_FROM, MAX_PER_F = 2, 8
SLOTS = 3
CONSTS = 21


def tok_uses(t):
    return [("xt", t, 0), ("xt", t, 1), ("tok", t)]


def ffn_in_uses(tiles):
    out = [("w1", 0)]
    for t in range(tiles):
        out += ([("w1", t + 1)] if t + 1 < tiles else []) + [("tt", t)]
    return out


def tail_uses(new, tiles):
    out = [("zt1", 0), ("zt1", 1)] if new else []
    out += [("bt", 3)] if tiles == NT else []
    out += [("att", 0), ("att", 1)]
    out += [("qk", 0), ("qk", 1)] if new else []
    out += [("wo", t) for t in range(tiles)]
    out += [("qk", 2), ("qk", 3)] + [("v", t) for t in range(NT)] if new else []
    return out + [("zt2", 0), ("zt2", 1), ("rt",)] + ffn_in_uses(tiles)


def attention_uses(new):
    out = []
    for c in range(CHUNKS):
        if new and c % 4 == 1:
            out += tok_uses(c // 4)
        if c % 4 == 2 and c > 4:
            out.append(("bt", c // 4 - 1))
    return out


W2_USES = [("w2", f) for f in range(NF)]
PRO_ORDER = (
    [("ws", 0), ("ws", 1), ("wt",), ("wrep",)] + [("wtok", k) for k in range(KX)]
    + [("czt", 0), ("czt", 1), ("ck",), ("cv",)]
    + [u for t in range(NT) for u in tok_uses(t)] + tail_uses(True, 1)
)
BODY_ORDER = W2_USES + attention_uses(True) + tail_uses(True, NT)
LAST_ORDER = W2_USES + attention_uses(False) + tail_uses(False, NT)
BODY_USES = len(BODY_ORDER)
assert BODY_USES % SLOTS == 0 and S_USES % SLOTS == 0
OFFSET = {"pro": {u: n for n, u in enumerate(PRO_ORDER)},
          "body": {u: n + len(PRO_ORDER) for n, u in enumerate(BODY_ORDER)},
          "last": {u: n + len(PRO_ORDER) for n, u in enumerate(LAST_ORDER)},
          "end": {u: n + len(PRO_ORDER) + len(LAST_ORDER) - BODY_USES for n, u in enumerate(W2_USES)}}


def wait(eng, sem, value):
    if isinstance(value, int) and value <= 0:
        return
    eng.wait_ge(sem, value)


def first(b):
    return isinstance(b, int) and b == 0


def brought_up(nb):
    return ("pro", 0) if first(nb) else ("body", nb - 1)


def tail_of(b):
    if isinstance(b, int):
        return ("pro", 0) if b == 0 else ("body", b - 1) if b < B else ("last", B - 1)
    return ("body", b - 1)


def units_of(c):
    n = S_EXP + sum(len(EXP_UNITS[k % NT]) for k in range(c))
    return [(n + i, j, w) for i, (j, w) in enumerate(EXP_UNITS[c % NT])]


class Steps:

    def __init__(self, eng, sem):
        self.eng, self.sem, self.base, self.n = eng, sem, 0, 0

    def __call__(self, ins):
        self.n += 1
        ins.then_inc(self.sem, 1)
        self.eng.wait_ge(self.sem, self.base + self.n)

    def loop(self, turn, per):
        self.start = self.n
        self.base, self.n = self.start + turn * per, 0

    def end(self, turns, per):
        assert self.n == per, (self.n, per)
        self.base, self.n = 0, self.start + turns * per


def build(nc, x, cls_tok, weight, wsum, WQ, WK, WV, WO, rw, rb, w1, w2, lw, lb, out):
    ctx = ExitStack()
    with ctx:
        def sb(name, shape, dt=F32):
            return ctx.enter_context(nc.sbuf_tensor(name, shape, dt))

        def sem(name):
            return ctx.enter_context(nc.semaphore(name))

        bank = [ctx.enter_context(nc.psum_tensor(f"bank{i}", [P, 512], F32)) for i in range(8)]
        scratch = nc.dram_tensor("qk_parts", (3, 4 * P, S), BF16, kind="Internal").ap()

        ident = sb("ident", [P, P])
        identb = sb("identb", [P, P], BF16)
        maskq = sb("maskq", [P, P], BF16)
        maskk = sb("maskk", [P, P], BF16)
        spread4 = sb("spread4", [DD, P])
        headmask = sb("headmask", [P, HT, NH])
        lower = sb("lower", [P, NE, NE])
        onerow = sb("onerow", [1, P])
        minus_half = sb("minus_half", [P, NT])
        select = sb("select", [P, NH], BF16)
        w_sb = sb("w_sb", [P, HT, DD])
        wT = sb("wT", [DD, D])
        wtok = sb("wtok", [P, KX, D])
        wq = sb("wq", [P, HT, 2 * D])
        wv = sb("wv", [P, HT, D])
        wo = sb("wo", [P, HT, D])
        rw_sb = sb("rw_sb", [P, HT, NE])
        rb_sb = sb("rb_sb", [1, NE])
        w1_sb = sb("w1_sb", [P, HT, NE * RK])
        w2_sb = sb("w2_sb", [P, NC, F])
        lw_sb = sb("lw_sb", [P, NF, D])
        bias = sb("bias", [P, D])
        vcls = sb("vcls", [P, NH, DK + 1])
        kc = sb("kc", [P, HT])
        kblk = sb("kblk", [P, HT, NH])

        xin = sb("xin", [P, 2, IN * DD])
        xT = sb("xT", [P, 4, 4 * P])
        hn = sb("hn", [P, NT, D])
        hc = sb("hc", [P, NT, D])
        x1 = sb("x1", [P, NT, D])
        x1b = sb("x1b", [P, NT, D])
        z = sb("z", [P, NT, D])
        zT = sb("zT", [P, HT, S])
        aT = sb("aT", [P, HT, S])
        stats = sb("stats", [P, NT, 6])
        mv = sb("mv", [P, 3, NT])
        veps = sb("veps", [P, NT])
        rstd = sb("rstd", [P, NT])
        qk = sb("qk", [P, 4, S])
        parts = sb("parts", [P, 3, 4, S], BF16)
        qs = sb("qs", [P, NH, S], BF16)
        ks = sb("ks", [P, NH, S], BF16)
        va = sb("va", [P, NT, NH, 2 * DK])
        cs = sb("cs", [P, NT, NH])
        top = sb("top", [P, NT, NH])
        mhl = sb("mhl", [P, NT, 2 * NH], BF16)
        msum = sb("msum", [P, NT, NH])
        mT = sb("mT", [P, S], BF16)
        pcls = sb("pcls", [P, NT, NH])
        ocls = sb("ocls", [P, NT, NH, DK + 1])
        pt = sb("pt", [P, 2, 4, S])
        ot = sb("ot", [P, 2, S])
        num = sb("num", [P, NT, 4, DK + 1])
        rden = sb("rden", [P, NT, 4])
        at = sb("at", [P, NT, D])
        lg = sb("lg", [P, NT, NE])
        lmax = sb("lmax", [P, NT])
        lsum = sb("lsum", [P, NT])
        cmp1 = sb("cmp1", [P, NT, NE, NE])
        cmp2 = sb("cmp2", [P, NT, NE, NE])
        rank = sb("rank", [P, NT, NE])
        mw = sb("mw", [P, NT, NE])
        tm = sb("tm", [P, 2, NE * RK])
        tT = sb("tT", [P, NC, S])
        g = sb("g", [P, 3, S])

        wsT = g[:, 0, :].rearrange("p (a n) -> p a n", a=IN // P)
        ws_sb = g[:, 1, :].rearrange("p (a n) -> p a n", a=HT)
        spread = g[:, 2, :].rearrange("p (k n) -> p k n", k=4)
        wrep = ot[:, 0, 0:D]
        rest = tm

        s_full = [sem(f"s_full{i}") for i in range(SLOTS)]
        s_free = [sem(f"s_free{i}") for i in range(SLOTS)]
        d_full = [sem(f"d_full{i}") for i in range(SLOTS)]
        d_free = [sem(f"d_free{i}") for i in range(SLOTS)]
        tok_w, attn_w, cls_in, ffn_in, ffn_w, last_bias = (
            sem(n) for n in ("tok_w", "attn_w", "cls_in", "ffn_in", "ffn_w", "last_bias"))
        x_full = [sem(f"x_full{i}") for i in range(2)]
        consts = sem("consts")
        dve_step = sem("dve_step")
        identb_ready, stack_set, va_set = sem("identb_ready"), sem("stack_set"), sem("va_set")
        kblk_ready, vcls_ready = sem("kblk_ready"), sem("vcls_ready")
        hc_ready = sem("hc_ready")
        var_ready, rstd_ready = sem("var_ready"), sem("rstd_ready")
        z_ready = sem("z_ready")
        part_ready, third_ready = sem("part_ready"), sem("third_ready")
        scr_w, scr_r = sem("scr_w"), sem("scr_r")
        mhl_ready, cs_ready, pcls_ready, ocls_ready = (
            sem(n) for n in ("mhl_ready", "cs_ready", "pcls_ready", "ocls_ready"))
        qs_max = sem("qs_max")
        pv_used = sem("pv_used")
        pv_full, ot_ready = sem("pv_full"), sem("ot_ready")
        num_ready, at_ready = sem("num_ready"), sem("at_ready")
        x1b_ready = sem("x1b_ready")
        lexp = sem("lexp")
        g_used = sem("g_used")
        lin_full, out_ready, out_stored = sem("lin_full"), sem("out_ready"), sem("out_stored")

        def d_at(part, name, b):
            n = OFFSET[part][name]
            i, k = n % SLOTS, n // SLOTS
            return bank[5 + i], d_full[i], d_free[i], k if part == "pro" else b * (BODY_USES // SLOTS) + k

        def s_at(n, b):
            i, k = n % SLOTS, n // SLOTS
            return bank[i], s_full[i], s_free[i], b * (S_USES // SLOTS) + k

        def written(eng, part, name, b):
            ps, full, free, k = d_at(part, name, b)
            eng.wait_ge(full, k + 1)
            return ps, free

        def taken(eng, part, name, b):
            ps, full, free, k = d_at(part, name, b)
            eng.wait_ge(free, k + 1)

        def scored(eng, n, b):
            ps, full, free, k = s_at(n, b)
            eng.wait_ge(full, k + 1)
            return ps, free

        def score_taken(eng, n, b):
            ps, full, free, k = s_at(n, b)
            eng.wait_ge(free, k + 1)

        block = ctx.enter_context(nc.Block())

        @block.sync
        def _(sp):
            def load_x(b, t):
                if t >= 2:
                    written(sp, brought_up(b)[0], ("xt", t - 2, 1), brought_up(b)[1])
                elif not first(b):
                    written(sp, brought_up(b - 1)[0], ("xt", t + 2, 1), brought_up(b - 1)[1])
                sp.dma_start(xin[:, t % 2, :], x[b, t * P:(t + 1) * P, :]).then_inc(x_full[t % 2], 16)

            def stack(b):
                wait(sp, scr_r, 2 * len(Q_PART) * 16 * b)
                for p, (ready, count) in enumerate(((part_ready, 8 * b + 7), (part_ready, 8 * b + 8), (third_ready, 4 * b + 4))):
                    sp.wait_ge(ready, count)
                    sp.dma_start(scratch[p].rearrange("(a r) t -> r a t", r=P), parts[:, p, :, :]).then_inc(scr_w, 16)
                if not first(b):
                    scored(sp, S_USES - 1, b - 1)
                sp.wait_ge(scr_w, 3 * 16 * b + 48)
                for j in range(len(Q_PART)):
                    rows = slice(DK * j, DK * j + DK)
                    q_part = scratch[Q_PART[j]][0:2 * P].rearrange("(h d) t -> d h t", d=DK)
                    k_part = scratch[K_PART[j]][2 * P:4 * P].rearrange("(h d) t -> d h t", d=DK)
                    sp.dma_start(qs[rows, :, :], q_part).then_inc(scr_r, 16)
                    sp.dma_start(ks[rows, :, :], k_part).then_inc(scr_r, 16)

            def store(b):
                sp.wait_ge(out_ready, 4 * b + 5)
                sp.dma_start(out[b, 1:, :].rearrange("(t p) d -> p t d", p=P), x1b[:, :, :]).then_inc(out_stored, 16)

            sp.dma_start(ws_sb[:, :, :], wsum.rearrange("(a p) i -> p a i", p=P)).then_inc(tok_w, 16)
            sp.dma_start(w_sb[:, :, :], weight.rearrange("(a p) d -> p a d", p=P)).then_inc(tok_w, 16)
            sp.dma_start(hc[:, 0, :], cls_tok[0].broadcast_to([P, D])).then_inc(cls_in, 16)
            load_x(0, 0)
            load_x(0, 1)
            sp.dma_start(wq[:, :, 0:D], WQ.rearrange("(k p) n -> p k n", p=P)).then_inc(attn_w, 16)
            sp.dma_start(wq[:, :, D:2 * D], WK.rearrange("(k p) n -> p k n", p=P)).then_inc(attn_w, 16)
            sp.dma_start(wv[:, :, :], WV.rearrange("(k p) n -> p k n", p=P)).then_inc(attn_w, 16)
            sp.dma_start(wo[:, :, :], WO.rearrange("(k p) n -> p k n", p=P)).then_inc(attn_w, 16)
            sp.dma_start(rw_sb[:, :, :], rw.rearrange("(k p) n -> p k n", p=P)).then_inc(ffn_in, 16)
            sp.dma_start(rb_sb[:, :], rb.rearrange("(a n) -> a n", a=1)).then_inc(ffn_in, 16)
            for k in range(HT):
                sp.dma_start(w1_sb[:, k, :].rearrange("p (e r) -> p e r", r=RK),
                             w1[:, k * P:(k + 1) * P, :].rearrange("e p r -> p e r")).then_inc(ffn_in, 16)
            sp.dma_start(bias[:, :], lb.rearrange("(a n) -> a n", a=1).broadcast_to([P, D])).then_inc(last_bias, 16)
            load_x(0, 2)
            load_x(0, 3)
            sp.dma_start(w2_sb[:, :, :], w2.rearrange("e r f -> (e r) f").rearrange("(c p) f -> p c f", p=P)).then_inc(ffn_w, 16)
            sp.dma_start(lw_sb[:, :, :], lw.rearrange("(c p) n -> p c n", p=P)).then_inc(ffn_w, 16)
            stack(0)

            def turn(b, new=True):
                if new:
                    load_x(b + 1, 0)
                    load_x(b + 1, 1)
                if first(b):
                    sp.wait_ge(out_ready, 1)
                    sp.dma_start(out[:, 0, :], x1b[0:B, 0, :]).then_inc(out_stored, 16)
                else:
                    store(b - 1)
                if new:
                    load_x(b + 1, 2)
                    load_x(b + 1, 3)
                    stack(b + 1)

            turn(0)
            with sp.Fori(1, B - 1) as b:
                turn(b)
            turn(B - 1, False)
            store(B - 1)
            sp.wait_ge(out_stored, 16 * (B + 1))

        @block.gpsimd
        def _(pool):
            G = nc.gpsimd
            step = Steps(pool, consts)
            step(G.memset(ident[:, :], 0.0))
            step(G.affine_select(out=ident[:, :], in_=ident[:, :], compare_op=ALU.not_equal, fill=1.0, base=0,
                            pattern=[[-1, P]], channel_multiplier=1))
            step(G.memset(minus_half[:, :], -0.5))
            step(G.memset(onerow[:, :], 1.0))
            step(G.memset(spread[:, :, :], 1.0))
            step(G.memset(spread4[:, :], 0.0))
            step(G.affine_select(out=spread[:, :, :], in_=spread[:, :, :], compare_op=ALU.is_ge, fill=0.0, base=0,
                                 pattern=[[P, 4], [1, P]], channel_multiplier=-4))
            step(G.affine_select(out=spread[:, :, :], in_=spread[:, :, :], compare_op=ALU.is_ge, fill=0.0, base=3,
                            pattern=[[-P, 4], [-1, P]], channel_multiplier=4))
            by_d = spread4[:, :].rearrange("d (i k) -> d i k", k=DD)
            step(G.affine_select(out=by_d, in_=by_d, compare_op=ALU.not_equal, fill=1.0, base=0,
                            pattern=[[0, P // DD], [-1, DD]], channel_multiplier=1))
            step(G.memset(headmask[:, :, :], 1.0))
            step(G.affine_select(out=headmask[:, :, :], in_=headmask[:, :, :], compare_op=ALU.is_ge, fill=0.0, base=0,
                                 pattern=[[P, HT], [-DK, NH]], channel_multiplier=1))
            step(G.affine_select(out=headmask[:, :, :], in_=headmask[:, :, :], compare_op=ALU.is_ge, fill=0.0, base=DK - 1,
                            pattern=[[-P, HT], [DK, NH]], channel_multiplier=-1))
            step(G.memset(maskq[:, :], 0.0))
            step(G.memset(maskk[:, :], 0.0))
            step(G.affine_select(out=maskq[:, :], in_=maskq[:, :], compare_op=ALU.is_ge, fill=MASKED, base=0,
                            pattern=[[-1, P]], channel_multiplier=1))
            step(G.affine_select(out=maskk[:, :], in_=maskk[:, :], compare_op=ALU.is_ge, fill=MASKED, base=0,
                            pattern=[[1, P]], channel_multiplier=-1))
            step(G.memset(lower[:, :, :], 1.0))
            step(G.affine_select(out=lower[:, :, :], in_=lower[:, :, :], compare_op=ALU.is_gt, fill=0.0, base=0,
                            pattern=[[1, NE], [-1, NE]], channel_multiplier=0))
            sel = select[STACK:P, :]
            step(G.memset(sel, 0.0))
            step(G.affine_select(out=sel, in_=sel, compare_op=ALU.not_equal, fill=-1.0, base=0,
                                 pattern=[[-1, NH]], channel_multiplier=1))
            step(G.affine_select(out=sel, in_=sel, compare_op=ALU.not_equal, fill=-1.0, base=-NH,
                            pattern=[[-1, NH]], channel_multiplier=1))

            assert step.n == CONSTS

            def rsqrt(n, tiles):
                pool.wait_ge(var_ready, n + 1)
                G.tensor_tensor(rstd[:, 0:tiles], veps[:, 0:tiles], minus_half[:, 0:tiles], ALU.pow).then_inc(rstd_ready, 1)

            def third_parts(b):
                for j in range(4):
                    pool.wait_ge(part_ready, 8 * b + 2 * j + 2)
                    if j == 0:
                        wait(pool, scr_w, 48 * b)
                    G.tensor_tensor(parts[:, 2, j, :], rest[:, j % 2, :], parts[:, 1, j, :], ALU.subtract).then_inc(third_ready, 1)

            def cls_values(b):
                pool.wait_ge(pcls_ready, b + 1)
                if first(b):
                    pool.wait_ge(vcls_ready, 2)
                wait(pool, num_ready, 4 * b)
                G.tensor_tensor(ocls[:, :, :, :],
                                pcls[:, :, :].rearrange("p t (h a) -> p t h a", a=1).broadcast_to([P, NT, NH, DK + 1]),
                                vcls[:, :, :].rearrange("p (a h) d -> p a h d", a=1).broadcast_to([P, NT, NH, DK + 1]),
                                ALU.mult).then_inc(ocls_ready, 1)

            def add_bias(part, b, j, tiles):
                taken(pool, part, ("wo", tiles - 1), b)
                wait(pool, out_stored, 16 * j)
                if first(j):
                    pool.wait_ge(last_bias, 16)
                G.tensor_tensor(x1b[:, 0:tiles, :], x1[:, 0:tiles, :],
                                bias[:, :].rearrange("p (a d) -> p a d", a=1).broadcast_to([P, tiles, D]),
                                ALU.add).then_inc(x1b_ready, 1)

            rsqrt(0, 1)
            rsqrt(1, NT)
            rsqrt(2, 1)
            third_parts(0)
            add_bias("pro", 0, 0, 1)

            def turn(part, b, new=True):
                cls_values(b)
                if new:
                    rsqrt(2 * b + 3, NT)
                rsqrt(2 * b + 4 if new else 2 * b + 3, NT)
                if new:
                    third_parts(b + 1)
                add_bias(part, b, b + 1, NT)

            turn("body", 0)
            with pool.Fori(1, B - 1) as b:
                turn("body", b)
            turn("last", B - 1, False)

        @block.scalar
        def _(act):
            A = nc.scalar

            def copy(part, name, b, dst, src):
                ps, free = written(act, part, name, b)
                A.activation(dst, src(ps), ACT.Copy).then_inc(free, 1)

            def tok(part, b, t):
                copy(part, ("xt", t, 0), b, xT[:, 2 * (t % 2), :], lambda ps: ps[:, :])
                copy(part, ("tok", t), b, hn[:, t, :], lambda ps: ps[:, 0:D])

            def transposed(part, name, b, dst, tiles):
                for ht in range(HT):
                    copy(part, (name, ht), b, dst[:, ht, 0:tiles * P], lambda ps: ps[:, 0:tiles * P])

            def tail(part, b, j, new, tiles):
                if new:
                    transposed(part, "zt1", b, zT, NT)
                transposed(part, "att", b, aT, tiles)
                if new:
                    for i in range(4):
                        copy(part, ("qk", i), b, qk[:, i, :], lambda ps: ps[:, :])
                    if part == "pro":
                        act.wait_ge(va_set, 1)
                    for t in range(NT):
                        copy(part, ("v", t), b, va[:, t, :, 0:DK], lambda ps: ps[:, 0:D].rearrange("p (h d) -> p h d", d=DK))
                transposed(part, "zt2", b, zT, tiles)
                taken(act, part, ("rt",), b)
                A.activation(lg[:, 0:tiles, :], lg[:, 0:tiles, :], ACT.Exp).then_inc(lexp, 1)
                for t in range(tiles):
                    copy(part, ("tt", t), b, tT[:, :, t * P:(t + 1) * P], lambda ps: ps[:, :].rearrange("p (c n) -> p c n", c=NC))

            def gelus(part, b, n):
                for f in range(NF):
                    if f < 3:
                        wait(act, lin_full, b)
                    else:
                        act.wait_ge(g_used, (NF - 1) * b + f - 2)
                    ps, free = written(act, part, ("w2", f), b)
                    A.activation(g[:, f % 3, 0:n], ps[:, 0:n], ACT.Gelu).then_inc(free, 1)

            def exps(b, c):
                q, kt = (c - 2) // NT, (c - 2) % NT
                if kt == NT - 1:
                    wait(act, pv_full, 4 * b + q + 1)
                else:
                    wait(act, pv_used, (CHUNKS - 4) * b + (NT - 1) * q + kt + 1)
                n = S - P * (c % NT)
                for u, j, w in units_of(c):
                    ps, free = scored(act, u, b)
                    A.activation(pt[:, c % 2, j:j + w, 0:n], ps[:, 0:w * n].rearrange("p (h n) -> p h n", h=w),
                                 ACT.Exp, scale=DK ** -0.5).then_inc(free, 1)

            def take_group(b, q):
                act.wait_ge(pv_full, 4 * b + q + 1)
                wait(act, num_ready, 4 * b + q - 1)
                A.activation(ot[:, q % 2, :], bank[3 + q % 2][:, :], ACT.Copy).then_inc(ot_ready, 1)

            def copy_h(b):
                part, turn_ = tail_of(b)
                taken(act, part, ("wo", 0 if first(b) else NT - 1), turn_)
                A.activation(hc[:, :, :], hn[:, :, :], ACT.Copy).then_inc(hc_ready, 1)

            def turn(part, b, n, new=True):
                copy_h(b)
                gelus(part, b, n)
                act.wait_ge(cs_ready, b + 1)
                wait(act, ocls_ready, b)
                A.activation(pcls[:, :, :], cs[:, :, :], ACT.Exp, scale=DK ** -0.5).then_inc(pcls_ready, 1)
                for c in range(CHUNKS):
                    exps(b, c)
                    if new and c % 4 == 1:
                        tok(part, b, c // 4)
                    if c % 4 == 0 and c:
                        take_group(b, c // 4 - 1)
                take_group(b, 3)
                tail(part, b, b + 1, new, NT)

            for i in range(HT):
                copy("pro", ("ws", i), 0, wsT[:, i, :], lambda ps: ps[:, 0:D])
            copy("pro", ("wt",), 0, wT[:, :], lambda ps: ps[0:DD, 0:D])
            copy("pro", ("wrep",), 0, wrep, lambda ps: ps[:, 0:D])
            transposed("pro", "czt", 0, zT, 1)
            copy("pro", ("ck",), 0, kc[:, :], lambda ps: ps[:, 0:HT * P].rearrange("p (a n) -> p a n", n=P)[:, :, 0])
            copy("pro", ("cv",), 0, vcls[:, :, 0:DK], lambda ps: ps[:, 0:D].rearrange("p (h d) -> p h d", d=DK))
            for t in range(NT):
                tok("pro", 0, t)
            tail("pro", 0, 0, True, 1)
            turn("body", 0, P)
            with act.Fori(1, B - 1) as b:
                turn("body", b, S)
            turn("last", B - 1, S, False)
            gelus("end", B, S)

        @block.vector
        def _(dve):
            V = nc.vector
            step = Steps(dve, dve_step)

            def layer_norm(n, src, tiles, arrived=None):
                for t in range(tiles):
                    if arrived:
                        arrived(t)
                    ins = V.bn_stats(stats[:, t, :], src[:, t, :])
                step(ins)
                even, odd = stats[:, 0:tiles, 0:3], stats[:, 0:tiles, 3:6]
                mean, dif, var = mv[:, 0, 0:tiles], mv[:, 1, 0:tiles], mv[:, 2, 0:tiles]
                V.tensor_tensor(mean, even[:, :, 1], odd[:, :, 1], ALU.add)
                V.tensor_tensor(dif, even[:, :, 1], odd[:, :, 1], ALU.subtract)
                step(V.tensor_tensor(var, even[:, :, 2], odd[:, :, 2], ALU.add))
                V.tensor_scalar(mean, mean, 0.5, None, ALU.mult)
                V.tensor_scalar(var, var, 1.0 / D, EPS, ALU.mult, ALU.add)
                step(V.scalar_tensor_tensor(out=dif, in0=dif, scalar=0.25, in1=dif, op0=ALU.mult, op1=ALU.mult))
                V.tensor_tensor(veps[:, 0:tiles], var, dif, ALU.add).then_inc(var_ready, 1)
                dve.wait_ge(rstd_ready, n + 1)
                for t in range(tiles):
                    ins = V.tensor_scalar(z[:, t, :], src[:, t, :], mv[:, 0, t:t + 1], rstd[:, t:t + 1], ALU.subtract, ALU.mult)
                ins.then_inc(z_ready, 1)

            def tok(part, b, t):
                ps, free = written(dve, part, ("xt", t, 1), b)
                V.tensor_copy(xT[:, 2 * (t % 2) + 1, :], ps[:, :]).then_inc(free, 1)

            def split(part, b, nb, j):
                taken(dve, part, ("qk", j), b)
                if j == 0:
                    wait(dve, scr_w, 48 * nb)
                V.tensor_copy(parts[:, 0, j, :], qk[:, j, :]).then_inc(part_ready, 1)
                dve.wait_ge(part_ready, 8 * nb + 2 * j + 1)
                wait(dve, third_ready, 4 * nb + j - 1)
                step(V.tensor_tensor(rest[:, j % 2, :], qk[:, j, :], parts[:, 0, j, :], ALU.subtract))
                V.tensor_copy(parts[:, 1, j, :], rest[:, j % 2, :]).then_inc(part_ready, 1)

            def normalise(part, b, q):
                if q == 0:
                    dve.wait_ge(ocls_ready, b + 1)
                ps, free = written(dve, part, ("bt", q), b)
                group = ps[:, :].rearrange("p (t h d) -> p t h d", t=NT, h=4)
                wait(dve, at_ready, 4 * b + q)
                V.tensor_tensor(num[:, :, :, :], group[:, :, :, 0:DK + 1], ocls[:, :, 4 * q:4 * q + 4, :], ALU.add).then_inc(free, 1)
                taken(dve, part, ("bt", q), b)
                V.reciprocal(rden[:, :, :], num[:, :, :, DK]).then_inc(num_ready, 1)
                dve.wait_ge(num_ready, 4 * b + q + 1)
                o = at[:, :, 4 * DK * q:4 * DK * (q + 1)].rearrange("p t (h d) -> p t h d", h=4)
                r = rden[:, :, :].rearrange("p t (h a) -> p t h a", a=1).broadcast_to([P, NT, 4, DK])
                V.tensor_tensor(o, num[:, :, :, 0:DK], r, ALU.mult).then_inc(at_ready, 1)

            def router(part, b, j, tiles):
                ps, free = written(dve, part, ("rt",), b)
                logits = ps[:, 0:tiles * NE].rearrange("p (t e) -> p t e", e=NE)
                own_lg = lg[:, 0:tiles, :]

                def over_experts(a):
                    return a[:, 0:tiles].rearrange("p (t a) -> p t a", a=1).broadcast_to([P, tiles, NE])

                step(V.tensor_reduce(lmax[:, 0:tiles], logits, AX_X, ALU.max))
                V.tensor_tensor(own_lg, logits, over_experts(lmax), ALU.subtract).then_inc(free, 1)
                dve.wait_ge(lexp, j + 1)
                step(V.tensor_reduce(lsum[:, 0:tiles], own_lg, AX_X, ALU.add))
                step(V.reciprocal(lsum[:, 0:tiles], lsum[:, 0:tiles]))
                step(V.tensor_tensor(own_lg, own_lg, over_experts(lsum), ALU.mult))
                shape = [P, tiles, NE, NE]
                other = own_lg.rearrange("p t (a j) -> p t a j", a=1).broadcast_to(shape)
                own = own_lg.rearrange("p t (e a) -> p t e a", a=1).broadcast_to(shape)
                low = lower[:, :, :].rearrange("p (a e) j -> p a e j", a=1).broadcast_to(shape)
                gt, eq = cmp1[:, 0:tiles, :, :], cmp2[:, 0:tiles, :, :]
                V.tensor_tensor(gt, other, own, ALU.is_gt)
                step(V.tensor_tensor(eq, other, own, ALU.is_equal))
                step(V.tensor_tensor(eq, eq, low, ALU.mult))
                step(V.tensor_tensor(gt, gt, eq, ALU.add))
                step(V.tensor_reduce(rank[:, 0:tiles, :], gt, AX_X, ALU.add))
                step(V.scalar_tensor_tensor(out=mw[:, 0:tiles, :], in0=rank[:, 0:tiles, :], scalar=2.0,
                                            in1=own_lg, op0=ALU.is_lt, op1=ALU.mult))

            def tail(part, b, j, new, tiles):
                if tiles == NT:
                    normalise(part, b, 3)
                if new:
                    split(part, b, j, 0)
                    split(part, b, j, 1)
                for t in range(tiles):
                    if part != "pro" and t == 0:
                        dve.wait_ge(hc_ready, b + 1)
                        dve.wait_ge(x1b_ready, b + 1)
                    ps, free = written(dve, part, ("wo", t), b)
                    V.tensor_tensor(x1[:, t, :], ps[:, 0:D], hc[:, t, :], ALU.add).then_inc(free, 1)
                if new:
                    written(dve, part, ("zt1", 1), b)
                n = {"pro": 2, "last": 2 * B + 1}[part] if part != "body" else 2 * b + 4
                layer_norm(n, x1, tiles, lambda t: taken(dve, part, ("wo", t), b))
                if new:
                    split(part, b, j, 2)
                    split(part, b, j, 3)
                    dve.wait_ge(third_ready, 4 * j + 4)
                router(part, b, j, tiles)
                for t in range(tiles):
                    ps, free = written(dve, part, ("w1", t), b)
                    V.tensor_tensor(tm[:, t % 2, :].rearrange("p (e r) -> p e r", r=RK), ps[:, :].rearrange("p (e r) -> p e r", r=RK),
                                    mw[:, t, :].rearrange("p (e a) -> p e a", a=1).broadcast_to([P, NE, RK]), ALU.mult).then_inc(free, 1)

            def finish(b, tiles):
                dve.wait_ge(lin_full, b + 1)
                dve.wait_ge(x1b_ready, b + 1)
                for t in range(tiles):
                    V.tensor_tensor(x1b[:, t, :], bank[3 + t // 2][:, D * (t % 2):D * (t % 2 + 1)], x1b[:, t, :], ALU.add).then_inc(out_ready, 1)

            def maxima(b):
                ps, free = scored(dve, S_CLS, b)
                wait(dve, pcls_ready, b)
                V.tensor_copy(cs[:, :, :], ps[:, 0:NT * NH].rearrange("p (t h) -> p t h", h=NH)).then_inc(free, 1)
                for i, (qt, h, w) in enumerate(MAX_UNITS):
                    n = P * (qt + 1)
                    ps, free = scored(dve, S_MAX + i, b)
                    V.tensor_reduce(top[:, qt, h:h + w], ps[:, 0:w * n].rearrange("p (h n) -> p h n", h=w), AX_X, ALU.max).then_inc(free, 1)
                for u in (S_CLS, S_MT - 3, S_MT - 2, S_MT - 1):
                    score_taken(dve, u, b)
                hi, lo = mhl[:, :, 0:NH], mhl[:, :, NH:2 * NH]
                step(V.tensor_tensor(top[:, :, :], top[:, :, :], cs[:, :, :], ALU.max))
                step(V.tensor_copy(hi, top[:, :, :]))
                V.tensor_tensor(lo, top[:, :, :], hi, ALU.subtract).then_inc(mhl_ready, 1)
                dve.wait_ge(mhl_ready, b + 1)
                step(V.tensor_tensor(msum[:, :, :], hi, lo, ALU.add))
                V.tensor_tensor(cs[:, :, :], cs[:, :, :], msum[:, :, :], ALU.subtract).then_inc(cs_ready, 1)

            def max_rows(b):
                ps, free = scored(dve, S_MT, b)
                V.tensor_copy(mT[STACK:P, :], ps[STACK:P, :]).then_inc(free, 1)
                score_taken(dve, S_MT, b)
                V.tensor_copy(qs[STACK:P, :, :], mT[STACK:P, :].rearrange("p (a t) -> p a t", a=1).broadcast_to([P - STACK, NH, S])).then_inc(qs_max, 1)

            def turn(part, b, tiles, new=True):
                maxima(b)
                max_rows(b)
                finish(b, tiles)
                for c in range(CHUNKS):
                    if new and c % 4 == 1:
                        tok(part, b, c // 4)
                    if c % 4 == 2 and c > 4:
                        normalise(part, b, c // 4 - 1)
                if new:
                    layer_norm(2 * b + 3, hn, NT, lambda t: taken(dve, part, ("tok", t), b))
                tail(part, b, b + 1, new, NT)

            dve.wait_ge(consts, CONSTS)
            V.tensor_copy(identb[:, :], ident[:, :]).then_inc(identb_ready, 1)
            dve.wait_ge(cls_in, 16)
            layer_norm(0, hc, 1)
            V.memset(va[:, :, :, DK:DK + 1], 1.0)
            V.memset(va[:, :, :, DK + 1:2 * DK], 0.0).then_inc(va_set, 1)
            V.memset(vcls[:, :, DK:DK + 1], 1.0).then_inc(vcls_ready, 1)
            V.tensor_copy(ks[STACK:P, :, :], select[STACK:P, :].rearrange("p (h a) -> p h a", a=1).broadcast_to([P - STACK, NH, S])).then_inc(stack_set, 1)
            taken(dve, "pro", ("wrep",), 0)
            for k in range(KX):
                ps, free = written(dve, "pro", ("wtok", k), 0)
                V.tensor_tensor(wtok[:, k, :], ps[:, 0:D], wrep, ALU.mult).then_inc(free, 1)
            taken(dve, "pro", ("ck",), 0)
            for ht in range(HT):
                ins = V.tensor_scalar(kblk[:, ht, :], headmask[:, ht, :], kc[:, ht:ht + 1], None, ALU.mult)
            ins.then_inc(kblk_ready, 1)
            taken(dve, "pro", ("cv",), 0)
            V.tensor_copy(at[:, 0, :].rearrange("p (h d) -> p h d", d=DK), vcls[:, :, 0:DK]).then_inc(vcls_ready, 1)
            for t in range(NT):
                tok("pro", 0, t)
            layer_norm(1, hn, NT, lambda t: taken(dve, "pro", ("tok", t), 0))
            tail("pro", 0, 0, True, 1)
            before = step.n
            turn("body", 0, 1)
            per = step.n - before
            with dve.Fori(1, B - 1) as b:
                step.loop(b - 1, per)
                turn("body", b, NT)
            step.end(B - 2, per)
            turn("last", B - 1, NT, False)
            finish(B, NT)

        @block.tensor
        def _(pe):
            T = nc.tensor

            def d_bank(part, name, b):
                ps, full, free, k = d_at(part, name, b)
                wait(pe, free, k)
                return ps, full

            def s_bank(n, b):
                ps, full, free, k = s_at(n, b)
                wait(pe, free, k)
                return ps, full

            def transpose_tiles(part, name, b, src, tiles):
                for ht in range(HT):
                    ps, full = d_bank(part, (name, ht), b)
                    for t in range(tiles):
                        ins = T.transpose(ps[:, t * P:(t + 1) * P], src[:, t, ht * P:(ht + 1) * P], ident[:, :])
                    ins.then_inc(full, 1)

            def xt(part, b, t):
                nb = 0 if part == "pro" else b + 1
                pe.wait_ge(x_full[t % 2], 32 * nb + 16 * (t // 2) + 16)
                for half in range(2):
                    ps, full = d_bank(part, ("xt", t, half), b)
                    for k in range(4):
                        ins = T.transpose(ps[:, k * P:(k + 1) * P], xin[:, t % 2, (4 * half + k) * P:(4 * half + k + 1) * P], ident[:, :])
                    ins.then_inc(full, 1)

            def tok(part, b, t):
                taken(pe, part, ("xt", t, 0), b)
                taken(pe, part, ("xt", t, 1), b)
                ps, full = d_bank(part, ("tok", t), b)
                for k in range(KX):
                    ins = T.matmul(ps[:, 0:D], xT[:, 2 * (t % 2) + k // 4, (k % 4) * P:(k % 4 + 1) * P], wtok[:, k, :],
                                   start=(k == 0), stop=(k == KX - 1))
                ins.then_inc(full, 1)

            def project(part, name, b, lhs, rhs, width):
                ps, full = d_bank(part, name, b)
                for k in range(HT):
                    ins = T.matmul(ps[:, 0:width], lhs(k), rhs(k), start=(k == 0), stop=(k == HT - 1))
                ins.then_inc(full, 1)

            def qk_tile(part, b, j):
                project(part, ("qk", j), b, lambda k: wq[:, k, j * P:(j + 1) * P], lambda k: zT[:, k, :], S)

            def back(part, b, q):
                pe.wait_ge(ot_ready, 4 * b + q + 1)
                ps, full = d_bank(part, ("bt", q), b)
                for t in range(NT):
                    ins = T.transpose(ps[:, t * P:(t + 1) * P], ot[:, q % 2, t * P:(t + 1) * P], ident[:, :])
                ins.then_inc(full, 1)

            def both(part, name, b):
                taken(pe, part, (name, 0), b)
                taken(pe, part, (name, 1), b)

            def tail(part, b, new, tiles):
                if new:
                    pe.wait_ge(z_ready, 2 if part == "pro" else 2 * b + 4)
                    transpose_tiles(part, "zt1", b, z, NT)
                if tiles == NT:
                    back(part, b, 3)
                    pe.wait_ge(at_ready, 4 * b + 4)
                else:
                    pe.wait_ge(vcls_ready, 2)
                transpose_tiles(part, "att", b, at, tiles)
                if new:
                    both(part, "zt1", b)
                    qk_tile(part, b, 0)
                    qk_tile(part, b, 1)
                both(part, "att", b)
                for t in range(tiles):
                    project(part, ("wo", t), b, lambda k: aT[:, k, t * P:(t + 1) * P], lambda k: wo[:, k, :], D)
                if new:
                    qk_tile(part, b, 2)
                    qk_tile(part, b, 3)
                    for t in range(NT):
                        project(part, ("v", t), b, lambda k: zT[:, k, t * P:(t + 1) * P], lambda k: wv[:, k, :], D)
                pe.wait_ge(z_ready, 2 * b + 5 if part == "body" else {"pro": 3, "last": 2 * B + 2}[part])
                transpose_tiles(part, "zt2", b, z, tiles)
                both(part, "zt2", b)
                if part == "pro":
                    pe.wait_ge(ffn_in, 64)
                ps, full = d_bank(part, ("rt",), b)
                for t in range(tiles):
                    o = ps[:, t * NE:(t + 1) * NE]
                    for k in range(HT):
                        T.matmul(o, zT[:, k, t * P:(t + 1) * P], rw_sb[:, k, :], start=(k == 0), stop=False)
                    ins = T.matmul(o, onerow[:, :], rb_sb[:, :], start=False, stop=True)
                ins.then_inc(full, 1)
                for use in ffn_in_uses(tiles):
                    t = use[1]
                    if use[0] == "w1":
                        project(part, use, b, lambda k: zT[:, k, t * P:(t + 1) * P], lambda k: w1_sb[:, k, :], NE * RK)
                    else:
                        taken(pe, part, ("w1", t), b)
                        ps, full = d_bank(part, use, b)
                        for c in range(NC):
                            ins = T.transpose(ps[:, c * P:(c + 1) * P], tm[:, t % 2, c * P:(c + 1) * P], ident[:, :])
                        ins.then_inc(full, 1)

            def ffn_mid(part, b, f, n):
                if f == 0:
                    for t in range(n // P):
                        taken(pe, tail_of(b)[0], ("tt", t), tail_of(b)[1])
                    if first(b):
                        pe.wait_ge(ffn_w, 32)
                ps, full = d_bank(part, ("w2", f), b)
                for c in range(NC):
                    ins = T.matmul(ps[:, 0:n], w2_sb[:, c, f * P:(f + 1) * P], tT[:, c, 0:n], start=(c == 0), stop=(c == NC - 1))
                ins.then_inc(full, 1)

            def ffn_out(part, b, f, n):
                taken(pe, part, ("w2", f), b)
                if f == 0:
                    wait(pe, ot_ready, 4 * b)
                for t in range(n // P):
                    ins = T.matmul(bank[3 + t // 2][:, D * (t % 2):D * (t % 2 + 1)], g[:, f % 3, t * P:(t + 1) * P], lw_sb[:, f, :],
                                   start=(f == 0 and t % 2 == 0), stop=(f == NF - 1), skip_group_check=True)
                ins.then_inc(g_used if f < NF - 1 else lin_full, 1)

            def cls_scores(b):
                ps, full = s_bank(S_CLS, b)
                part, turn_ = brought_up(b)
                taken(pe, part, ("qk", 1), turn_)
                if first(b):
                    pe.wait_ge(kblk_ready, 1)
                for qt in range(NT):
                    for ht in range(HT):
                        ins = T.matmul(ps[:, qt * NH:(qt + 1) * NH], qk[:, ht, qt * P:(qt + 1) * P], kblk[:, ht, :],
                                       start=(ht == 0), stop=(ht == HT - 1))
                ins.then_inc(full, 1)

            def max_unit(b, i):
                qt, h0, w = MAX_UNITS[i]
                n = P * (qt + 1)
                ps, full = s_bank(S_MAX + i, b)
                if i == 0:
                    pe.wait_ge(scr_r, 2 * len(Q_PART) * 16 * (b + 1))
                for j in range(w):
                    T.matmul(ps[:, j * n:(j + 1) * n], qs[0:STACK, h0 + j, qt * P:(qt + 1) * P], ks[0:STACK, h0 + j, 0:n],
                             start=True, stop=False, skip_group_check=True)
                    ins = T.matmul(ps[:, (j + 1) * n - P:(j + 1) * n], identb[:, :], maskq[:, :],
                                   start=False, stop=True, skip_group_check=True)
                ins.then_inc(full, 1)

            def turn_maxima(b):
                pe.wait_ge(mhl_ready, b + 1)
                ps, full = s_bank(S_MT, b)
                for t in range(NT):
                    ins = T.matmul(ps[STACK:P, t * P:(t + 1) * P], mhl[:, t, :], identb[:, :], start=True, stop=True)
                ins.then_inc(full, 1)

            def exp_unit(b, c, u, j, w):
                kt, n = c % NT, S - P * (c % NT)
                ps, full = s_bank(u, b)
                for i in range(w):
                    h = 4 * (c // NT) + j + i
                    T.matmul(ps[:, i * n:(i + 1) * n], ks[:, h, kt * P:(kt + 1) * P], qs[:, h, kt * P:S],
                             start=True, stop=False, skip_group_check=True)
                    ins = T.matmul(ps[:, i * n:i * n + P], identb[:, :], maskk[:, :], start=False, stop=True, skip_group_check=True)
                ins.then_inc(full, 1)

            def values(b, c):
                q, kt = c // NT, c % NT
                n = S - P * kt
                for u, _, _ in units_of(c):
                    score_taken(pe, u, b)
                if kt == 0:
                    if q < 2:
                        pe.wait_ge(out_ready, 4 * b + 1)
                    else:
                        pe.wait_ge(ot_ready, 4 * b + q - 1)
                for j in range(4):
                    ins = T.matmul(bank[3 + q % 2][32 * j:32 * j + 32, P * kt:S], va[:, kt, 4 * q + j, :], pt[:, c % 2, j, 0:n],
                                   start=(kt == 0), stop=(kt == NT - 1), skip_group_check=True)
                ins.then_inc(pv_full if kt == NT - 1 else pv_used, 1)

            def turn(part, b, n, new=True):
                done = 0
                for f in range(NF):
                    ffn_mid(part, b, f, n)
                    if f:
                        ffn_out(part, b, f - 1, n)
                    if f == MAX_FROM:
                        cls_scores(b)
                    if f >= MAX_FROM:
                        for i in range(done, min(done + MAX_PER_F, len(MAX_UNITS))):
                            max_unit(b, i)
                        done += MAX_PER_F
                ffn_out(part, b, NF - 1, n)
                turn_maxima(b)
                if new:
                    xt(part, b, 0)
                pe.wait_ge(qs_max, b + 1)
                for c in range(CHUNKS):
                    for u, j, w in units_of(c):
                        exp_unit(b, c, u, j, w)
                    if c:
                        values(b, c - 1)
                    if new and c % 4 == 1:
                        if c > 1:
                            xt(part, b, c // 4)
                        tok(part, b, c // 4)
                    if c % 4 == 2 and c > 4:
                        back(part, b, c // 4 - 1)
                values(b, CHUNKS - 1)
                tail(part, b, new, NT)

            pe.wait_ge(consts, CONSTS)
            pe.wait_ge(identb_ready, 1)
            pe.wait_ge(tok_w, 32)
            for i in range(HT):
                ps, full = d_bank("pro", ("ws", i), 0)
                for a in range(HT):
                    ins = T.transpose(ps[:, a * P:(a + 1) * P], ws_sb[:, a, i * P:(i + 1) * P], ident[:, :])
                ins.then_inc(full, 1)
            ps, full = d_bank("pro", ("wt",), 0)
            for a in range(HT):
                ins = T.transpose(ps[0:DD, a * P:(a + 1) * P], w_sb[:, a, :], ident[:, :])
            ins.then_inc(full, 1)
            taken(pe, "pro", ("wt",), 0)
            ps, full = d_bank("pro", ("wrep",), 0)
            T.matmul(ps[:, 0:D], spread4[:, :], wT[:, :], start=True, stop=True).then_inc(full, 1)
            both("pro", "ws", 0)
            for k in range(KX):
                ps, full = d_bank("pro", ("wtok", k), 0)
                T.matmul(ps[:, 0:D], spread[:, k % 4, :], wsT[:, k // 4, :], start=True, stop=True).then_inc(full, 1)
            pe.wait_ge(z_ready, 1)
            transpose_tiles("pro", "czt", 0, z, 1)
            both("pro", "czt", 0)
            pe.wait_ge(attn_w, 64)
            ps, full = d_bank("pro", ("ck",), 0)
            for ht in range(HT):
                for k in range(HT):
                    ins = T.matmul(ps[:, ht * P:(ht + 1) * P], wq[:, k, D + ht * P:D + (ht + 1) * P], zT[:, k, 0:P],
                                   start=(k == 0), stop=(k == HT - 1))
            ins.then_inc(full, 1)
            project("pro", ("cv",), 0, lambda k: zT[:, k, 0:P], lambda k: wv[:, k, :], D)
            for i in range(KX):
                taken(pe, "pro", ("wtok", i), 0)
            for t in range(NT):
                xt("pro", 0, t)
                tok("pro", 0, t)
            tail("pro", 0, True, 1)
            pe.wait_ge(stack_set, 1)
            turn("body", 0, P)
            with pe.Fori(1, B - 1) as b:
                turn("body", b, S)
            turn("last", B - 1, S, False)
            for f in range(NF):
                ffn_mid("end", B, f, S)
                if f:
                    ffn_out("end", B, f - 1, S)
            ffn_out("end", B, NF - 1, S)


INPUTS = ["x", "cls_tok", "L0_tok_weight", "L0_tok_weighted_sum", "L0_attn_WQ", "L0_attn_WK", "L0_attn_WV", "L0_attn_WO",
          "L0_ffn_router_w", "L0_ffn_router_b", "L0_ffn_w1", "L0_ffn_w2", "L0_ffn_lin2_w", "L0_ffn_lin2_b"]


def kernel(**inputs):
    import numpy as np
    import concourse.bacc as bacc
    from concourse.bass_utils import run_bass_kernel_spmd

    nc = bacc.Bacc("TRN2", target_bir_lowering=False, num_devices=1)
    arrays, args = {}, []
    for name in INPUTS:
        a = np.ascontiguousarray(inputs[name])
        if name == "x":
            a = a.reshape(B, S, IN * DD)
        arrays["in_" + name] = a
        args.append(nc.dram_tensor("in_" + name, a.shape, mybir.dt.from_np(a.dtype), kind="ExternalInput").ap())
    args.append(nc.dram_tensor("out_h", (B, S + 1, D), F32, kind="ExternalOutput").ap())
    build(nc, *args)
    r = run_bass_kernel_spmd(nc, [arrays], core_ids=[0])
    return r.results[0]["out_h"]
```

```python
from contextlib import ExitStack

import concourse.bass as bass
from concourse import mybir

ALU = mybir.AluOpType
ACT = mybir.ActivationFunctionType
AX_X = mybir.AxisListType.X
F32 = mybir.dt.float32
F32R = mybir.dt.float32r
BF16 = mybir.dt.bfloat16

P = 128
B, S, IN, DD = 8, 512, 256, 4
D, NH, DK = 256, 16, 16
NE, RK, F = 8, 64, 1024
NT = S // P
KX = IN * DD // P
HT = D // P
NC = NE * RK // P
NF = F // P
CHUNKS = 4 * NT
EPS = 1e-5
MASKED = -1e30
Q_PART = (0, 0, 1, 1, 0, 2)
K_PART = (0, 1, 0, 1, 2, 0)
STACK = DK * len(Q_PART)

MAX_UNITS = [(qt, h, n) for qt, n in ((0, 4), (1, 2), (2, 1), (3, 1)) for h in range(0, NH, n)]
EXP_UNITS = [[(j, 1) for j in range(4)], [(j, 1) for j in range(4)], [(0, 2), (2, 2)], [(0, 4)]]
N_EXP = 4 * sum(len(u) for u in EXP_UNITS)
S_CLS, S_W1, S_MAX = 0, 1, NT
S_MT = S_MAX + len(MAX_UNITS)
S_EXP = S_MT + 1
S_USES = S_EXP + N_EXP
MAX_FROM = 1
SLOTS = 3
CONSTS = 20


def tok_uses(t):
    return [("xt", t, 0), ("xt", t, 1), ("tok", t)]


UP_USES = [("zt1", 0), ("zt1", 1), ("qk", 0)]


def tail_uses(new, tiles):
    def filler(*uses):
        return list(uses) if new else []

    out = filler(("qk", 1)) + ([("bt", 3)] if tiles == NT else [])
    out += filler(("qk", 2)) + [("att", 0), ("att", 1)] + filler(("qk", 3))
    out += [("wo", t) for t in range(0, tiles, 2)]
    out += filler(("v", 0), ("v", 2)) + [("zt2", 0), ("zt2", 1), ("lt",)]
    if tiles < NT:
        return out + [("w1", 0), ("rt",), ("tt", 0)]
    return out + [("rt",), ("w1", 3)] + [("tt", t) for t in range(tiles)]


def attention_uses(new):
    out = tok_uses(0) + tok_uses(1)[0:2] if new else []
    for q in range(4):
        if new and q + 1 < NT:
            out.append(("tok", q + 1))
        elif new:
            out += [("zt1", 0), ("zt1", 1)]
        if q:
            out.append(("bt", q - 1))
        if new and q + 2 < NT:
            out += tok_uses(q + 2)[0:2]
    return out + ([("qk", 0)] if new else [])


W2_USES = [("w2", f) for f in range(NF)]
PRO_ORDER = (
    [("ws", 0), ("ws", 1), ("wt",), ("wrep",)] + [("wtok", k) for k in range(KX)]
    + [("czt", 0), ("czt", 1), ("ck",), ("cv",)]
    + [u for t in range(NT) for u in tok_uses(t)] + UP_USES + tail_uses(True, 1)
)
BODY_ORDER = W2_USES + attention_uses(True) + tail_uses(True, NT)
LAST_ORDER = W2_USES + attention_uses(False) + tail_uses(False, NT)
BODY_USES = len(BODY_ORDER)
assert BODY_USES % SLOTS == 0 and S_USES % SLOTS == 0
OFFSET = {"pro": {u: n for n, u in enumerate(PRO_ORDER)},
          "body": {u: n + len(PRO_ORDER) for n, u in enumerate(BODY_ORDER)},
          "last": {u: n + len(PRO_ORDER) for n, u in enumerate(LAST_ORDER)},
          "end": {u: n + len(PRO_ORDER) + len(LAST_ORDER) - BODY_USES for n, u in enumerate(W2_USES)}}


def wait(eng, sem, value):
    if isinstance(value, int) and value <= 0:
        return
    eng.wait_ge(sem, value)


def first(b):
    return isinstance(b, int) and b == 0


def brought_up(nb):
    return ("pro", 0) if first(nb) else ("body", nb - 1)


def tail_of(b):
    if isinstance(b, int):
        return ("pro", 0) if b == 0 else ("body", b - 1) if b < B else ("last", B - 1)
    return ("body", b - 1)


def units_of(c):
    n = S_EXP + sum(len(EXP_UNITS[k % NT]) for k in range(c))
    return [(n + i, j, w) for i, (j, w) in enumerate(EXP_UNITS[c % NT])]


class Steps:

    def __init__(self, eng, sem):
        self.eng, self.sem, self.base, self.n = eng, sem, 0, 0

    def __call__(self, ins):
        self.n += 1
        ins.then_inc(self.sem, 1)
        self.eng.wait_ge(self.sem, self.base + self.n)

    def loop(self, turn, per):
        self.start = self.n
        self.base, self.n = self.start + turn * per, 0

    def end(self, turns, per):
        assert self.n == per, (self.n, per)
        self.base, self.n = 0, self.start + turns * per


def build(nc, x, cls_tok, weight, wsum, WQ, WK, WV, WO, rw, rb, w1, w2, lw, lb, out):
    ctx = ExitStack()
    with ctx:
        def sb(name, shape, dt=F32):
            return ctx.enter_context(nc.sbuf_tensor(name, shape, dt))

        def sem(name):
            return ctx.enter_context(nc.semaphore(name))

        def overlay(*layouts):
            out = []
            for layout in layouts:
                with ExitStack() as own:
                    keep = ctx if layout is layouts[-1] else own
                    out += [keep.enter_context(nc.sbuf_tensor(name, shape, dt)) for name, shape, dt in layout]
            return out

        bank = [ctx.enter_context(nc.psum_tensor(f"bank{i}", [P, 512], F32)) for i in range(8)]
        scratch = nc.dram_tensor("qk_parts", (3, 4 * P, S), BF16, kind="Internal").ap()

        ident = sb("ident", [P, P])
        identb = sb("identb", [P, P], BF16)
        maskq = sb("maskq", [P, P], BF16)
        maskk = sb("maskk", [P, P], BF16)
        headmask = sb("headmask", [P, HT, NH])
        lower = sb("lower", [P, NE, NE])
        minus_half = sb("minus_half", [P, NT])
        select = sb("select", [P, NH], BF16)
        wtok = sb("wtok", [P, KX, D])
        wq = sb("wq", [P, HT, 2 * D])
        wv = sb("wv", [P, HT, D])
        wo = sb("wo", [P, HT, D])
        rw_sb = sb("rw_sb", [P, HT, NE])
        rb_sb = sb("rb_sb", [P, NE])
        w1_sb = sb("w1_sb", [P, HT, NE * RK])
        w2_hi, w2_lo = sb("w2_hi", [P, NC, F], F32R), sb("w2_lo", [P, NC, F], F32R)
        lw_hi, lw_lo = sb("lw_hi", [P, NF, D], F32R), sb("lw_lo", [P, NF, D], F32R)
        bias = sb("bias", [P, D])
        vcls = sb("vcls", [P, NH, DK + 1])
        kc = sb("kc", [P, HT])
        kblk = sb("kblk", [P, HT, NH])

        xin = sb("xin", [P, 2, IN * DD])
        xT, parts = overlay([("xT", [P, 4, 4 * P], F32)], [("parts", [P, 3, 4, S], BF16)])
        hn = sb("hn", [P, NT, D])
        hc = sb("hc", [P, NT, D])
        x1 = sb("x1", [P, NT, D])
        x1b = sb("x1b", [P, NT, D])
        z = sb("z", [P, NT, D])
        zT = sb("zT", [P, HT, S])
        aT = sb("aT", [P, HT, S])
        stats = sb("stats", [P, NT, 6])
        mv = sb("mv", [P, 3, NT])
        veps = sb("veps", [P, NT])
        shift = sb("shift", [P, NT])
        rstd = sb("rstd", [P, NT])
        w2_in, lw_in, qs, ks = overlay([("w2_in", [P, NC, F], F32), ("lw_in", [P, NF, D], F32)],
                                       [("qs", [P, NH, S], BF16), ("ks", [P, NH, S], BF16)])
        va = sb("va", [P, NT, NH, 2 * DK])
        cs = sb("cs", [P, NT, NH])
        top = sb("top", [P, NT, NH])
        mhl = sb("mhl", [P, NT, 2 * NH], BF16)
        msum = sb("msum", [P, NT, NH])
        mT = sb("mT", [P, S], BF16)
        pcls = sb("pcls", [P, NT, NH])
        ocls = sb("ocls", [P, NT, NH, DK + 1])
        tT_hi, tT_lo, pt = overlay([("tT_hi", [P, NC, S], F32R), ("tT_lo", [P, NC, S], F32R)], [("pt", [P, 2, 4, S], F32)])
        wsT, ws_sb, spread, wrep, spread4, w_sb, wT, g, g_hi, g_lo, ot, at, qT = overlay(
            [("wsT", [P, IN // P, D], F32), ("ws_sb", [P, HT, IN], F32),
             ("spread", [P, 4, P], F32),
             ("wrep", [P, D], F32),
             ("spread4", [DD, P], F32),
             ("w_sb", [P, HT, DD], F32), ("wT", [DD, D], F32)],
            [("g", [P, 2, S], F32), ("g_hi", [P, 2, S], F32R), ("g_lo", [P, 2, S], F32R)],
            [("ot", [P, 2, S], F32), ("at", [P, NT, D], F32), ("qT", [P, HT, S], F32)])
        num = sb("num", [P, NT, 4, DK + 1])
        rden = sb("rden", [P, NT, 4])
        lgT = sb("lgT", [P, S])
        lg = sb("lg", [P, 2, NT, NE])
        lmax = sb("lmax", [P, NT])
        lsum = sb("lsum", [P, NT])
        cmp1 = sb("cmp1", [P, NT, NE, NE])
        cmp2 = sb("cmp2", [P, NT, NE, NE])
        rank = sb("rank", [P, NT, NE])
        mw = sb("mw", [P, NT, NE])
        tm = sb("tm", [P, 2, NE * RK])
        rest = tm

        s_full = [sem(f"s_full{i}") for i in range(SLOTS)]
        s_free = [sem(f"s_free{i}") for i in range(SLOTS)]
        d_full = [sem(f"d_full{i}") for i in range(SLOTS)]
        d_free = [sem(f"d_free{i}") for i in range(SLOTS)]
        tok_w, attn_w, cls_in, ffn_in, ffn_w, last_bias = (
            sem(n) for n in ("tok_w", "attn_w", "cls_in", "ffn_in", "ffn_w", "last_bias"))
        x_full = [sem(f"x_full{i}") for i in range(2)]
        consts = sem("consts")
        dve_step = sem("dve_step")
        identb_ready, stack_set, va_set = sem("identb_ready"), sem("stack_set"), sem("va_set")
        kblk_ready, vcls_ready = sem("kblk_ready"), sem("vcls_ready")
        hc_ready = sem("hc_ready")
        var_ready, rstd_ready = sem("var_ready"), sem("rstd_ready")
        z_ready = sem("z_ready")
        shift_ready, z_late_ready = sem("shift_ready"), sem("z_late_ready")
        first_ready, second_ready, third_ready = sem("first_ready"), sem("second_ready"), sem("third_ready")
        scr_w, scr_r = sem("scr_w"), sem("scr_r")
        mhl_ready, cs_ready, pcls_ready, ocls_ready = (
            sem(n) for n in ("mhl_ready", "cs_ready", "pcls_ready", "ocls_ready"))
        qs_max = sem("qs_max")
        pv_used = sem("pv_used")
        pv_full, ot_ready = sem("pv_full"), sem("ot_ready")
        num_ready, at_ready = sem("num_ready"), sem("at_ready")
        x1b_ready = sem("x1b_ready")
        w2_hi_ready, lw_hi_ready, ffn_split = sem("w2_hi_ready"), sem("lw_hi_ready"), sem("ffn_split")
        tT_hi_ready = sem("tT_hi_ready")
        g_hi_ready, g_lo_ready = sem("g_hi_ready"), sem("g_lo_ready")
        lexp = sem("lexp")
        g_used = sem("g_used")
        lin_full, out_ready, out_stored = sem("lin_full"), sem("out_ready"), sem("out_stored")

        def d_at(part, name, b):
            n = OFFSET[part][name]
            i, k = n % SLOTS, n // SLOTS
            return bank[5 + i], d_full[i], d_free[i], k if part == "pro" else b * (BODY_USES // SLOTS) + k

        def s_at(n, b):
            i, k = n % SLOTS, n // SLOTS
            if not first(b) or n >= S_MAX:
                k -= 1
            return bank[i], s_full[i], s_free[i], b * (S_USES // SLOTS) + k

        def written(eng, part, name, b):
            ps, full, free, k = d_at(part, name, b)
            eng.wait_ge(full, k + 1)
            return ps, free

        def taken(eng, part, name, b):
            ps, full, free, k = d_at(part, name, b)
            eng.wait_ge(free, k + 1)

        def scored(eng, n, b):
            ps, full, free, k = s_at(n, b)
            eng.wait_ge(full, k + 1)
            return ps, free

        def score_taken(eng, n, b):
            ps, full, free, k = s_at(n, b)
            eng.wait_ge(free, k + 1)

        def w1_at(part, t, b):
            if part == "pro" or t == NT - 1:
                return d_at(part, ("w1", t), b)
            return s_at(t, B) if part == "last" else s_at(S_W1 + t, b + 1)

        block = ctx.enter_context(nc.Block())

        @block.sync
        def _(sp):
            def load_x(b, t):
                if t >= 2:
                    written(sp, brought_up(b)[0], ("xt", t - 2, 1), brought_up(b)[1])
                elif not first(b):
                    written(sp, brought_up(b - 1)[0], ("xt", t + 2, 1), brought_up(b - 1)[1])
                sp.dma_start(xin[:, t % 2, :], x[b, t * P:(t + 1) * P, :]).then_inc(x_full[t % 2], 16)

            def stack(b):
                wait(sp, scr_r, 2 * len(Q_PART) * 16 * b)
                for p, ready in enumerate((first_ready, second_ready, third_ready)):
                    sp.wait_ge(ready, 4 * b + 4)
                    sp.dma_start(scratch[p].rearrange("(a r) t -> r a t", r=P), parts[:, p, :, :]).then_inc(scr_w, 16)
                if first(b):
                    sp.wait_ge(ffn_split, 1)
                else:
                    scored(sp, S_USES - 1, b - 1)
                sp.wait_ge(scr_w, 3 * 16 * b + 48)
                for j in range(len(Q_PART)):
                    rows = slice(DK * j, DK * j + DK)
                    q_part = scratch[Q_PART[j]][0:2 * P].rearrange("(h d) t -> d h t", d=DK)
                    k_part = scratch[K_PART[j]][2 * P:4 * P].rearrange("(h d) t -> d h t", d=DK)
                    sp.dma_start(qs[rows, :, :], q_part).then_inc(scr_r, 16)
                    sp.dma_start(ks[rows, :, :], k_part).then_inc(scr_r, 16)

            def store(b):
                sp.wait_ge(out_ready, 4 * b + 5)
                sp.dma_start(out[b, 1:, :].rearrange("(t p) d -> p t d", p=P), x1b[:, :, :]).then_inc(out_stored, 16)

            sp.dma_start(ws_sb[:, :, :], wsum.rearrange("(a p) i -> p a i", p=P)).then_inc(tok_w, 16)
            sp.dma_start(w_sb[:, :, :], weight.rearrange("(a p) d -> p a d", p=P)).then_inc(tok_w, 16)
            sp.dma_start(hc[:, 0, :], cls_tok[0].broadcast_to([P, D])).then_inc(cls_in, 16)
            load_x(0, 0)
            load_x(0, 1)
            sp.dma_start(wq[:, :, 0:D], WQ.rearrange("(k p) n -> p k n", p=P)).then_inc(attn_w, 16)
            sp.dma_start(wq[:, :, D:2 * D], WK.rearrange("(k p) n -> p k n", p=P)).then_inc(attn_w, 16)
            sp.dma_start(wv[:, :, :], WV.rearrange("(k p) n -> p k n", p=P)).then_inc(attn_w, 16)
            sp.dma_start(wo[:, :, :], WO.rearrange("(k p) n -> p k n", p=P)).then_inc(attn_w, 16)
            sp.dma_start(rw_sb[:, :, :], rw.rearrange("(k p) n -> p k n", p=P)).then_inc(ffn_in, 16)
            sp.dma_start(rb_sb[:, :], rb.rearrange("(a n) -> a n", a=1).broadcast_to([P, NE])).then_inc(ffn_in, 16)
            for k in range(HT):
                sp.dma_start(w1_sb[:, k, :].rearrange("p (e r) -> p e r", r=RK),
                             w1[:, k * P:(k + 1) * P, :].rearrange("e p r -> p e r")).then_inc(ffn_in, 16)
            sp.dma_start(bias[:, :], lb.rearrange("(a n) -> a n", a=1).broadcast_to([P, D])).then_inc(last_bias, 16)
            load_x(0, 2)
            load_x(0, 3)
            sp.dma_start(w2_in[:, :, :], w2.rearrange("e r f -> (e r) f").rearrange("(c p) f -> p c f", p=P)).then_inc(ffn_w, 16)
            sp.dma_start(lw_in[:, :, :], lw.rearrange("(c p) n -> p c n", p=P)).then_inc(ffn_w, 16)
            stack(0)

            def turn(b, new=True):
                if new:
                    load_x(b + 1, 0)
                    load_x(b + 1, 1)
                if first(b):
                    sp.wait_ge(out_ready, 1)
                    sp.dma_start(out[:, 0, :], x1b[0:B, 0, :]).then_inc(out_stored, 16)
                else:
                    store(b - 1)
                if new:
                    load_x(b + 1, 2)
                    load_x(b + 1, 3)
                    stack(b + 1)

            turn(0)
            with sp.Fori(1, B - 1) as b:
                turn(b)
            turn(B - 1, False)
            store(B - 1)
            sp.wait_ge(out_stored, 16 * (B + 1))

        @block.gpsimd
        def _(pool):
            G = nc.gpsimd
            step = Steps(pool, consts)
            step(G.memset(ident[:, :], 0.0))
            step(G.affine_select(out=ident[:, :], in_=ident[:, :], compare_op=ALU.not_equal, fill=1.0, base=0,
                            pattern=[[-1, P]], channel_multiplier=1))
            step(G.memset(minus_half[:, :], -0.5))
            step(G.memset(spread[:, :, :], 1.0))
            step(G.memset(spread4[:, :], 0.0))
            step(G.affine_select(out=spread[:, :, :], in_=spread[:, :, :], compare_op=ALU.is_ge, fill=0.0, base=0,
                                 pattern=[[P, 4], [1, P]], channel_multiplier=-4))
            step(G.affine_select(out=spread[:, :, :], in_=spread[:, :, :], compare_op=ALU.is_ge, fill=0.0, base=3,
                            pattern=[[-P, 4], [-1, P]], channel_multiplier=4))
            by_d = spread4[:, :].rearrange("d (i k) -> d i k", k=DD)
            step(G.affine_select(out=by_d, in_=by_d, compare_op=ALU.not_equal, fill=1.0, base=0,
                            pattern=[[0, P // DD], [-1, DD]], channel_multiplier=1))
            step(G.memset(headmask[:, :, :], 1.0))
            step(G.affine_select(out=headmask[:, :, :], in_=headmask[:, :, :], compare_op=ALU.is_ge, fill=0.0, base=0,
                                 pattern=[[P, HT], [-DK, NH]], channel_multiplier=1))
            step(G.affine_select(out=headmask[:, :, :], in_=headmask[:, :, :], compare_op=ALU.is_ge, fill=0.0, base=DK - 1,
                            pattern=[[-P, HT], [DK, NH]], channel_multiplier=-1))
            step(G.memset(maskq[:, :], 0.0))
            step(G.memset(maskk[:, :], 0.0))
            step(G.affine_select(out=maskq[:, :], in_=maskq[:, :], compare_op=ALU.is_ge, fill=MASKED, base=0,
                            pattern=[[-1, P]], channel_multiplier=1))
            step(G.affine_select(out=maskk[:, :], in_=maskk[:, :], compare_op=ALU.is_ge, fill=MASKED, base=0,
                            pattern=[[1, P]], channel_multiplier=-1))
            step(G.memset(lower[:, :, :], 1.0))
            step(G.affine_select(out=lower[:, :, :], in_=lower[:, :, :], compare_op=ALU.is_gt, fill=0.0, base=0,
                            pattern=[[1, NE], [-1, NE]], channel_multiplier=0))
            sel = select[STACK:P, :]
            step(G.memset(sel, 0.0))
            step(G.affine_select(out=sel, in_=sel, compare_op=ALU.not_equal, fill=-1.0, base=0,
                                 pattern=[[-1, NH]], channel_multiplier=1))
            step(G.affine_select(out=sel, in_=sel, compare_op=ALU.not_equal, fill=-1.0, base=-NH,
                            pattern=[[-1, NH]], channel_multiplier=1))

            assert step.n == CONSTS

            def rsqrt(n, tiles):
                pool.wait_ge(var_ready, n + 1)
                G.tensor_tensor(rstd[:, 0:tiles], veps[:, 0:tiles], minus_half[:, 0:tiles], ALU.pow).then_inc(rstd_ready, 1)

            def third_parts(b, tiles):
                for j in tiles:
                    pool.wait_ge(second_ready, 4 * b + j + 1)
                    if j == 0:
                        wait(pool, scr_w, 48 * b)
                    G.tensor_tensor(parts[:, 2, j, :], rest[:, j % 2, :], parts[:, 1, j, :], ALU.subtract).then_inc(third_ready, 1)

            def cls_values(b):
                pool.wait_ge(pcls_ready, b + 1)
                if first(b):
                    pool.wait_ge(vcls_ready, 2)
                wait(pool, num_ready, 4 * b)
                G.tensor_tensor(ocls[:, :, :, :],
                                pcls[:, :, :].rearrange("p t (h a) -> p t h a", a=1).broadcast_to([P, NT, NH, DK + 1]),
                                vcls[:, :, :].rearrange("p (a h) d -> p a h d", a=1).broadcast_to([P, NT, NH, DK + 1]),
                                ALU.mult).then_inc(ocls_ready, 1)

            def add_bias(part, b, j, tiles):
                taken(pool, part, ("wo", 2 * ((tiles - 1) // 2)), b)
                wait(pool, out_stored, 16 * j)
                if first(j):
                    pool.wait_ge(last_bias, 16)
                G.tensor_tensor(x1b[:, 0:tiles, :], x1[:, 0:tiles, :],
                                bias[:, :].rearrange("p (a d) -> p a d", a=1).broadcast_to([P, tiles, D]),
                                ALU.add).then_inc(x1b_ready, 1)

            rsqrt(0, 1)
            rsqrt(1, NT)
            third_parts(0, (0, 1))
            rsqrt(2, 1)
            third_parts(0, (2, 3))
            add_bias("pro", 0, 0, 1)

            def turn(part, b, new=True):
                cls_values(b)
                if new:
                    rsqrt(2 * b + 3, NT)
                    third_parts(b + 1, (0, 1))
                rsqrt(2 * b + 4 if new else 2 * b + 3, NT)
                if new:
                    third_parts(b + 1, (2, 3))
                add_bias(part, b, b + 1, NT)

            turn("body", 0)
            with pool.Fori(1, B - 1) as b:
                turn("body", b)
            turn("last", B - 1, False)

        @block.scalar
        def _(act):
            A = nc.scalar

            def copy(part, name, b, dst, src):
                ps, free = written(act, part, name, b)
                A.activation(dst, src(ps), ACT.Copy).then_inc(free, 1)

            def first_part(part, b, nb, i):
                if i == 0:
                    wait(act, scr_w, 48 * nb)
                ps, free = written(act, part, ("qk", i), b)
                if i < HT:
                    A.activation(qT[:, i, :], ps[:, :], ACT.Copy)
                A.activation(parts[:, 0, i, :], ps[:, :], ACT.Copy).then_inc(first_ready, 1)

            def second_part(part, b, i):
                taken(act, part, ("qk", i), b)
                A.activation(parts[:, 1, i, :], rest[:, i % 2, :], ACT.Copy).then_inc(second_ready, 1)

            def v_tiles(part, b, t):
                copy(part, ("v", t), b, va[:, t:t + 2, :, 0:DK], lambda ps: ps[:, :].rearrange("p (t h d) -> p t h d", t=2, d=DK))

            def tT_tile(part, b, t):
                ps, free = written(act, part, ("tt", t), b)
                A.activation(tT_hi[:, :, t * P:(t + 1) * P], ps[:, :].rearrange("p (c n) -> p c n", c=NC),
                             ACT.Copy).then_inc(tT_hi_ready, 1)

            def tail(part, b, nb, new, tiles):
                if new:
                    first_part(part, b, nb, 0)
                    first_part(part, b, nb, 1)
                    second_part(part, b, 0)
                    first_part(part, b, nb, 2)
                    second_part(part, b, 1)
                copy(part, ("att", 0), b, aT[:, 0, 0:tiles * P], lambda ps: ps[:, 0:tiles * P])
                if new:
                    second_part(part, b, 2)
                    first_part(part, b, nb, 3)
                    if part == "pro":
                        act.wait_ge(va_set, 1)
                    v_tiles(part, b, 0)
                    second_part(part, b, 3)
                if tiles == NT:
                    act.wait_ge(shift_ready, b + 1)
                    for t in (2, 3):
                        ins = A.activation(z[:, t, :], x1[:, t, :], ACT.Identity, scale=rstd[:, t:t + 1], bias=shift[:, t:t + 1])
                    ins.then_inc(z_late_ready, 1)
                if new:
                    v_tiles(part, b, 2)
                copy(part, ("zt2", 0), b, aT[:, 0, 0:tiles * P], lambda ps: ps[:, 0:tiles * P])
                copy(part, ("lt",), b, lgT[0:NE, 0:tiles * P], lambda ps: ps[0:NE, 0:tiles * P])
                taken(act, part, ("rt",), b)
                A.activation(lg[:, 1, 0:tiles, :], lg[:, 1, 0:tiles, :], ACT.Exp).then_inc(lexp, 1)
                for t in range(tiles):
                    tT_tile(part, b, t)

            def gelus(part, b, n):
                for f in range(NF):
                    if f < 2:
                        wait(act, lin_full, b)
                    else:
                        act.wait_ge(g_used, (NF - 1) * b + f - 1)
                    ps, free = written(act, part, ("w2", f), b)
                    A.activation(g[:, f % 2, 0:n], ps[:, 0:n], ACT.Gelu).then_inc(free, 1)
                    taken(act, part, ("w2", f), b)
                    A.activation(g_hi[:, f % 2, 0:n], g[:, f % 2, 0:n], ACT.Copy).then_inc(g_hi_ready, 1)

            def exps(b, c):
                q, kt = (c - 2) // NT, (c - 2) % NT
                if kt == NT - 1:
                    wait(act, pv_full, 4 * b + q + 1)
                else:
                    wait(act, pv_used, (CHUNKS - 4) * b + (NT - 1) * q + kt + 1)
                n = S - P * (c % NT)
                for u, j, w in units_of(c):
                    ps, free = scored(act, u, b)
                    A.activation(pt[:, c % 2, j:j + w, 0:n], ps[:, 0:w * n].rearrange("p (h n) -> p h n", h=w),
                                 ACT.Exp, scale=DK ** -0.5).then_inc(free, 1)

            def copy_h(b):
                part, turn_ = tail_of(b)
                taken(act, part, ("wo", 0 if first(b) else NT - 2), turn_)
                A.activation(hc[:, :, :], hn[:, :, :], ACT.Copy).then_inc(hc_ready, 1)

            def turn(part, b, n, new=True):
                copy_h(b)
                gelus(part, b, n)
                act.wait_ge(cs_ready, b + 1)
                wait(act, ocls_ready, b)
                A.activation(pcls[:, :, :], cs[:, :, :], ACT.Exp, scale=DK ** -0.5).then_inc(pcls_ready, 1)
                for c in range(CHUNKS):
                    exps(b, c)
                tail(part, b, b + 1, new, NT)

            for i in range(HT):
                copy("pro", ("ws", i), 0, wsT[:, i, :], lambda ps: ps[:, 0:D])
            copy("pro", ("wt",), 0, wT[:, :], lambda ps: ps[0:DD, 0:D])
            copy("pro", ("wrep",), 0, wrep[:, :], lambda ps: ps[:, 0:D])
            for ht in range(HT):
                copy("pro", ("czt", ht), 0, zT[:, ht, 0:P], lambda ps: ps[:, 0:P])
            copy("pro", ("ck",), 0, kc[:, :], lambda ps: ps[:, 0:HT * P].rearrange("p (a n) -> p a n", n=P)[:, :, 0])
            copy("pro", ("cv",), 0, vcls[:, :, 0:DK], lambda ps: ps[:, 0:D].rearrange("p (h d) -> p h d", d=DK))
            act.wait_ge(ffn_w, 32)
            for c in range(NC):
                A.activation(w2_hi[:, c, :], w2_in[:, c, :], ACT.Copy).then_inc(w2_hi_ready, 1)
            A.activation(lw_hi[:, :, :], lw_in[:, :, :], ACT.Copy).then_inc(lw_hi_ready, 1)
            tail("pro", 0, 0, True, 1)
            turn("body", 0, P)
            with act.Fori(1, B - 1) as b:
                turn("body", b, S)
            turn("last", B - 1, S, False)
            gelus("end", B, S)

        @block.vector
        def _(dve):
            V = nc.vector
            step = Steps(dve, dve_step)

            def layer_norm(n, src, tiles, shared=False):
                even, odd = stats[:, 0:tiles, 0:3], stats[:, 0:tiles, 3:6]
                mean, dif, var = mv[:, 0, 0:tiles], mv[:, 1, 0:tiles], mv[:, 2, 0:tiles]
                V.tensor_tensor(mean, even[:, :, 1], odd[:, :, 1], ALU.add)
                V.tensor_tensor(dif, even[:, :, 1], odd[:, :, 1], ALU.subtract)
                step(V.tensor_tensor(var, even[:, :, 2], odd[:, :, 2], ALU.add))
                V.tensor_scalar(mean, mean, 0.5, None, ALU.mult)
                V.tensor_scalar(var, var, 1.0 / D, EPS, ALU.mult, ALU.add)
                step(V.scalar_tensor_tensor(out=dif, in0=dif, scalar=0.25, in1=dif, op0=ALU.mult, op1=ALU.mult))
                V.tensor_tensor(veps[:, 0:tiles], var, dif, ALU.add).then_inc(var_ready, 1)
                dve.wait_ge(rstd_ready, n + 1)
                if shared:
                    V.scalar_tensor_tensor(out=shift[:, :], in0=mean, scalar=-1.0, in1=rstd[:, :], op0=ALU.mult,
                                           op1=ALU.mult).then_inc(shift_ready, 1)
                for t in range(2 if shared else tiles):
                    ins = V.tensor_scalar(z[:, t, :], src[:, t, :], mv[:, 0, t:t + 1], rstd[:, t:t + 1], ALU.subtract, ALU.mult)
                ins.then_inc(z_ready, 1)

            def copy(part, name, b, dst, src):
                ps, free = written(dve, part, name, b)
                V.tensor_copy(dst, src(ps)).then_inc(free, 1)

            def take_x(part, b, t, half):
                copy(part, ("xt", t, half), b, xT[:, 2 * (t % 2) + half, :], lambda ps: ps[:, :])

            def take_h(part, b, t):
                if part != "pro" and t == 0:
                    dve.wait_ge(hc_ready, b + 1)
                copy(part, ("tok", t), b, hn[:, t, :], lambda ps: ps[:, 0:D])
                taken(dve, part, ("tok", t), b)
                step(V.bn_stats(stats[:, t, :], hn[:, t, :]))

            def split(part, b, nb, j):
                dve.wait_ge(first_ready, 4 * nb + j + 1)
                wait(dve, third_ready, 4 * nb + j - 1)
                ps, free = written(dve, part, ("qk", j), b)
                V.tensor_tensor(rest[:, j % 2, :], ps[:, :], parts[:, 0, j, :], ALU.subtract).then_inc(free, 1)

            def take_z(part, b):
                copy(part, ("zt1", 0), b, zT[:, 0, :], lambda ps: ps[:, :])
                copy(part, ("zt1", 1), b, zT[:, 1, :], lambda ps: ps[:, :])

            def take_group(b, q):
                dve.wait_ge(pv_full, 4 * b + q + 1)
                V.tensor_copy(ot[:, q % 2, :], bank[3 + q % 2][:, :]).then_inc(ot_ready, 1)

            def normalise(part, b, q):
                if q == 0:
                    dve.wait_ge(ocls_ready, b + 1)
                ps, free = written(dve, part, ("bt", q), b)
                group = ps[:, :].rearrange("p (t h d) -> p t h d", t=NT, h=4)
                wait(dve, at_ready, 4 * b + q)
                V.tensor_tensor(num[:, :, :, :], group[:, :, :, 0:DK + 1], ocls[:, :, 4 * q:4 * q + 4, :], ALU.add).then_inc(free, 1)
                taken(dve, part, ("bt", q), b)
                V.reciprocal(rden[:, :, :], num[:, :, :, DK]).then_inc(num_ready, 1)
                dve.wait_ge(num_ready, 4 * b + q + 1)
                o = at[:, :, 4 * DK * q:4 * DK * (q + 1)].rearrange("p t (h d) -> p t h d", h=4)
                r = rden[:, :, :].rearrange("p t (h a) -> p t h a", a=1).broadcast_to([P, NT, 4, DK])
                V.tensor_tensor(o, num[:, :, :, 0:DK], r, ALU.mult).then_inc(at_ready, 1)

            def router(part, b, j, tiles):
                ps, free = written(dve, part, ("rt",), b)
                logits = ps[:, 0:tiles * P].rearrange("p (t e) -> p t e", e=P)[:, :, 0:NE]
                own_lg, less_max = lg[:, 0, 0:tiles, :], lg[:, 1, 0:tiles, :]

                def over_experts(a):
                    return a[:, 0:tiles].rearrange("p (t a) -> p t a", a=1).broadcast_to([P, tiles, NE])

                bias_lg = rb_sb[:, :].rearrange("p (a e) -> p a e", a=1).broadcast_to([P, tiles, NE])
                if first(j):
                    dve.wait_ge(ffn_in, 64)
                step(V.tensor_tensor(own_lg, logits, bias_lg, ALU.add))
                step(V.tensor_reduce(lmax[:, 0:tiles], own_lg, AX_X, ALU.max))
                V.tensor_tensor(less_max, own_lg, over_experts(lmax), ALU.subtract).then_inc(free, 1)
                shape = [P, tiles, NE, NE]
                other = own_lg.rearrange("p t (a j) -> p t a j", a=1).broadcast_to(shape)
                own = own_lg.rearrange("p t (e a) -> p t e a", a=1).broadcast_to(shape)
                low = lower[:, :, :].rearrange("p (a e) j -> p a e j", a=1).broadcast_to(shape)
                gt, eq = cmp1[:, 0:tiles, :, :], cmp2[:, 0:tiles, :, :]
                V.tensor_tensor(gt, other, own, ALU.is_gt)
                step(V.tensor_tensor(eq, other, own, ALU.is_equal))
                step(V.tensor_tensor(eq, eq, low, ALU.mult))
                step(V.tensor_tensor(gt, gt, eq, ALU.add))
                dve.wait_ge(lexp, j + 1)
                V.tensor_reduce(rank[:, 0:tiles, :], gt, AX_X, ALU.add)
                step(V.tensor_reduce(lsum[:, 0:tiles], less_max, AX_X, ALU.add))
                V.reciprocal(lsum[:, 0:tiles], lsum[:, 0:tiles])
                step(V.scalar_tensor_tensor(out=mw[:, 0:tiles, :], in0=rank[:, 0:tiles, :], scalar=2.0,
                                            in1=less_max, op0=ALU.is_lt, op1=ALU.mult))
                step(V.tensor_tensor(mw[:, 0:tiles, :], mw[:, 0:tiles, :], over_experts(lsum), ALU.mult))

            def tT_rest(part, b, j, t):
                dve.wait_ge(tT_hi_ready, 1 if part == "pro" else 4 * j - 2 + t)
                ps, free = written(dve, part, ("tt", t), b)
                cols = slice(t * P, (t + 1) * P)
                V.tensor_tensor(tT_lo[:, :, cols], ps[:, :].rearrange("p (c n) -> p c n", c=NC), tT_hi[:, :, cols].bitcast(F32),
                                ALU.subtract).then_inc(free, 1)

            def g_rest(b, f, n):
                dve.wait_ge(g_hi_ready, NF * b + f + 1)
                V.tensor_tensor(g_lo[:, f % 2, 0:n], g[:, f % 2, 0:n], g_hi[:, f % 2, 0:n].bitcast(F32), ALU.subtract).then_inc(g_lo_ready, 1)

            def take_cls(nb):
                wait(dve, pcls_ready, nb)
                ps, free = scored(dve, S_CLS, nb)
                V.tensor_copy(cs[:, :, :], ps[:, 0:NT * NH].rearrange("p (t h) -> p t h", h=NH)).then_inc(free, 1)

            def tail(part, b, j, new, tiles):
                if tiles == NT:
                    take_group(b, 3)
                if new:
                    split(part, b, j, 0)
                    split(part, b, j, 1)
                if tiles == NT:
                    normalise(part, b, 3)
                if new:
                    split(part, b, j, 2)
                copy(part, ("att", 1), b, aT[:, 1, 0:tiles * P], lambda ps: ps[:, 0:tiles * P])
                if new:
                    split(part, b, j, 3)
                for t in range(0, tiles, 2):
                    w = min(2, tiles)
                    if part != "pro" and t == 0:
                        dve.wait_ge(hc_ready, b + 1)
                        dve.wait_ge(x1b_ready, b + 1)
                    ps, free = written(dve, part, ("wo", t), b)
                    V.tensor_tensor(x1[:, t:t + w, :], ps[:, 0:w * D].rearrange("p (t d) -> p t d", t=w), hc[:, t:t + w, :],
                                    ALU.add).then_inc(free, 1)
                    taken(dve, part, ("wo", t), b)
                    for i in range(t, t + w):
                        ins = V.bn_stats(stats[:, i, :], x1[:, i, :])
                    step(ins)
                n = {"pro": 2, "last": 2 * B + 1}[part] if part != "body" else 2 * b + 4
                layer_norm(n, x1, tiles, tiles == NT)
                copy(part, ("zt2", 1), b, aT[:, 1, 0:tiles * P], lambda ps: ps[:, 0:tiles * P])
                if new:
                    take_cls(j)
                    dve.wait_ge(third_ready, 4 * j + 4)
                router(part, b, j, tiles)
                for t in range(tiles):
                    if t >= 2:
                        written(dve, part, ("tt", t - 2), b)
                    ps, full, free, k = w1_at(part, t, b)
                    dve.wait_ge(full, k + 1)
                    V.tensor_tensor(tm[:, t % 2, :].rearrange("p (e r) -> p e r", r=RK), ps[:, :].rearrange("p (e r) -> p e r", r=RK),
                                    mw[:, t, :].rearrange("p (e a) -> p e a", a=1).broadcast_to([P, NE, RK]), ALU.mult).then_inc(free, 1)
                    if t >= 2:
                        tT_rest(part, b, j, t - 2)
                for t in range(max(tiles - 2, 0), tiles):
                    tT_rest(part, b, j, t)

            def finish(b, tiles):
                dve.wait_ge(lin_full, b + 1)
                dve.wait_ge(x1b_ready, b + 1)
                for t in range(tiles):
                    V.tensor_tensor(x1b[:, t, :], bank[3 + t // 2][:, D * (t % 2):D * (t % 2 + 1)], x1b[:, t, :], ALU.add).then_inc(out_ready, 1)

            def maxima(b, tiles):
                for i, (qt, h, w) in enumerate(MAX_UNITS):
                    if i % 8 == 0:
                        g_rest(b, i // 8, tiles * P)
                    n = P * (qt + 1)
                    ps, free = scored(dve, S_MAX + i, b)
                    V.tensor_reduce(top[:, qt, h:h + w], ps[:, 0:w * n].rearrange("p (h n) -> p h n", h=w), AX_X, ALU.max).then_inc(free, 1)
                for u in (S_CLS, S_MT - 3, S_MT - 2, S_MT - 1):
                    score_taken(dve, u, b)
                hi, lo = mhl[:, :, 0:NH], mhl[:, :, NH:2 * NH]
                step(V.tensor_tensor(top[:, :, :], top[:, :, :], cs[:, :, :], ALU.max))
                step(V.tensor_copy(hi, top[:, :, :]))
                V.tensor_tensor(lo, top[:, :, :], hi, ALU.subtract).then_inc(mhl_ready, 1)
                dve.wait_ge(mhl_ready, b + 1)
                step(V.tensor_tensor(msum[:, :, :], hi, lo, ALU.add))
                V.tensor_tensor(cs[:, :, :], cs[:, :, :], msum[:, :, :], ALU.subtract).then_inc(cs_ready, 1)
                g_rest(b, NF - 2, tiles * P)

            def max_rows(b):
                ps, free = scored(dve, S_MT, b)
                V.tensor_copy(mT[STACK:P, :], ps[STACK:P, :]).then_inc(free, 1)
                score_taken(dve, S_MT, b)

            def spread_rows(q):
                V.tensor_copy(qs[STACK:P, 4 * q:4 * q + 4, :],
                              mT[STACK:P, :].rearrange("p (a t) -> p a t", a=1).broadcast_to([P - STACK, 4, S])).then_inc(qs_max, 1)

            def turn(part, b, tiles, new=True):
                maxima(b, tiles)
                max_rows(b)
                spread_rows(0)
                g_rest(b, NF - 1, tiles * P)
                if new:
                    take_x(part, b, 0, 0)
                    take_x(part, b, 0, 1)
                spread_rows(1)
                finish(b, tiles)
                spread_rows(2)
                spread_rows(3)
                if new:
                    take_h(part, b, 0)
                    take_x(part, b, 1, 0)
                    take_x(part, b, 1, 1)
                for q in range(4):
                    if q:
                        take_group(b, q - 1)
                    if new and q + 1 < NT:
                        take_h(part, b, q + 1)
                    if new and q + 2 == NT:
                        layer_norm(2 * b + 3, hn, NT)
                    if new and q + 1 == NT:
                        take_z(part, b)
                    if q:
                        normalise(part, b, q - 1)
                    if new and q + 2 < NT:
                        take_x(part, b, q + 2, 0)
                        take_x(part, b, q + 2, 1)
                tail(part, b, b + 1, new, NT)

            dve.wait_ge(consts, CONSTS)
            V.tensor_copy(identb[:, :], ident[:, :]).then_inc(identb_ready, 1)
            dve.wait_ge(cls_in, 16)
            step(V.bn_stats(stats[:, 0, :], hc[:, 0, :]))
            layer_norm(0, hc, 1)
            V.memset(lgT[:, :], 0.0)
            V.memset(va[:, :, :, DK:DK + 1], 1.0)
            V.memset(va[:, :, :, DK + 1:2 * DK], 0.0).then_inc(va_set, 1)
            V.memset(vcls[:, :, DK:DK + 1], 1.0).then_inc(vcls_ready, 1)
            taken(dve, "pro", ("wrep",), 0)

            def w2_rest(c):
                dve.wait_ge(w2_hi_ready, c + 1)
                V.tensor_tensor(w2_lo[:, c, :], w2_in[:, c, :], w2_hi[:, c, :].bitcast(F32), ALU.subtract)

            for k in range(KX):
                ps, free = written(dve, "pro", ("wtok", k), 0)
                V.tensor_tensor(wtok[:, k, :], ps[:, 0:D], wrep[:, :], ALU.mult).then_inc(free, 1)
            taken(dve, "pro", ("ck",), 0)
            for ht in range(HT):
                ins = V.tensor_scalar(kblk[:, ht, :], headmask[:, ht, :], kc[:, ht:ht + 1], None, ALU.mult)
            ins.then_inc(kblk_ready, 1)
            taken(dve, "pro", ("cv",), 0)
            V.tensor_copy(at[:, 0, :].rearrange("p (h d) -> p h d", d=DK), vcls[:, :, 0:DK]).then_inc(vcls_ready, 1)
            for t in range(NT):
                take_x("pro", 0, t, 0)
                take_x("pro", 0, t, 1)
                take_h("pro", 0, t)
                if t == 2:
                    w2_rest(0)
                    w2_rest(1)
            layer_norm(1, hn, NT)
            take_z("pro", 0)
            w2_rest(2)
            w2_rest(3)
            dve.wait_ge(lw_hi_ready, 1)
            V.tensor_tensor(lw_lo[:, :, :], lw_in[:, :, :], lw_hi[:, :, :].bitcast(F32), ALU.subtract).then_inc(ffn_split, 1)
            dve.wait_ge(ffn_split, 1)
            V.tensor_copy(ks[STACK:P, :, :], select[STACK:P, :].rearrange("p (h a) -> p h a", a=1).broadcast_to([P - STACK, NH, S])).then_inc(stack_set, 1)
            tail("pro", 0, 0, True, 1)
            before = step.n
            turn("body", 0, 1)
            per = step.n - before
            with dve.Fori(1, B - 1) as b:
                step.loop(b - 1, per)
                turn("body", b, NT)
            step.end(B - 2, per)
            turn("last", B - 1, NT, False)
            for f in range(NF):
                g_rest(B, f, S)
            finish(B, NT)

        @block.tensor
        def _(pe):
            T = nc.tensor

            def d_bank(part, name, b):
                ps, full, free, k = d_at(part, name, b)
                wait(pe, free, k)
                return ps, full

            def s_bank(n, b):
                ps, full, free, k = s_at(n, b)
                wait(pe, free, k)
                return ps, full

            def transpose_tiles(part, name, b, src, tiles):
                for ht in range(HT):
                    ps, full = d_bank(part, (name, ht), b)
                    for t in range(tiles):
                        ins = T.transpose(ps[:, t * P:(t + 1) * P], src[:, t, ht * P:(ht + 1) * P], ident[:, :])
                    ins.then_inc(full, 1)

            def xt(part, b, t, half):
                nb = 0 if part == "pro" else b + 1
                if half == 0:
                    pe.wait_ge(x_full[t % 2], 32 * nb + 16 * (t // 2) + 16)
                ps, full = d_bank(part, ("xt", t, half), b)
                for k in range(4):
                    ins = T.transpose(ps[:, k * P:(k + 1) * P], xin[:, t % 2, (4 * half + k) * P:(4 * half + k + 1) * P], ident[:, :])
                ins.then_inc(full, 1)

            def tok(part, b, t, quarter):
                if quarter % 2 == 0:
                    taken(pe, part, ("xt", t, quarter // 2), b)
                if quarter == 0:
                    ps, full = d_bank(part, ("tok", t), b)
                else:
                    ps, full, _, _ = d_at(part, ("tok", t), b)
                for k in (2 * quarter, 2 * quarter + 1):
                    ins = T.matmul(ps[:, 0:D], xT[:, 2 * (t % 2) + k // 4, (k % 4) * P:(k % 4 + 1) * P], wtok[:, k, :],
                                   start=(k == 0), stop=(k == KX - 1), skip_group_check=True)
                if quarter == 3:
                    ins.then_inc(full, 1)

            def project(part, name, b, lhs, rhs, width):
                ps, full = d_bank(part, name, b)
                for k in range(HT):
                    ins = T.matmul(ps[:, 0:width], lhs(k), rhs(k), start=(k == 0), stop=(k == HT - 1))
                ins.then_inc(full, 1)

            def bring_up(part, b):
                def zt1(ht):
                    ps, full = d_bank(part, ("zt1", ht), b)
                    for t in range(NT):
                        ins = T.transpose(ps[:, t * P:(t + 1) * P], z[:, t, ht * P:(ht + 1) * P], ident[:, :])
                    ins.then_inc(full, 1)

                def qk0():
                    both(part, "zt1", b)
                    qk_tile(part, b, 0)

                def after_norm():
                    pe.wait_ge(z_ready, 2 if part == "pro" else 2 * b + 4)
                    zt1(0)

                return [after_norm, lambda: zt1(1), qk0]

            def nothing():
                pass

            def qk_tile(part, b, j):
                project(part, ("qk", j), b, lambda k: wq[:, k, j * P:(j + 1) * P], lambda k: zT[:, k, :], S)

            def back(part, b, q):
                pe.wait_ge(ot_ready, 4 * b + q + 1)
                ps, full = d_bank(part, ("bt", q), b)
                for t in range(NT):
                    ins = T.transpose(ps[:, t * P:(t + 1) * P], ot[:, q % 2, t * P:(t + 1) * P], ident[:, :])
                ins.then_inc(full, 1)

            def both(part, name, b):
                taken(pe, part, (name, 0), b)
                taken(pe, part, (name, 1), b)

            def pair(part, name, b, t0, tiles, src, w, between=lambda: None):
                ps, full = d_bank(part, (name, t0), b)
                for t in range(t0, min(t0 + 2, tiles)):
                    for k in range(HT):
                        ins = T.matmul(ps[:, D * (t - t0):D * (t - t0 + 1)], src[:, k, t * P:(t + 1) * P], w[:, k, :],
                                       start=(k == 0), stop=(k == HT - 1), skip_group_check=True)
                        if (t, k) != (min(t0 + 2, tiles) - 1, HT - 1):
                            between()
                ins.then_inc(full, 1)
                between()

            def w1_tile(part, b, t):
                ps, full, free, used = w1_at(part, t, b)
                wait(pe, free, used)
                for k in range(HT):
                    ins = T.matmul(ps[:, :], aT[:, k, t * P:(t + 1) * P], w1_sb[:, k, :], start=(k == 0), stop=(k == HT - 1))
                ins.then_inc(full, 1)

            def weighted(part, b, t):
                _, _, weighted_tile, k = w1_at(part, t, b)
                pe.wait_ge(weighted_tile, k + 1)
                ps, full = d_bank(part, ("tt", t), b)
                for c in range(NC):
                    ins = T.transpose(ps[:, c * P:(c + 1) * P], tm[:, t % 2, c * P:(c + 1) * P], ident[:, :])
                ins.then_inc(full, 1)

            def tail(part, b, new, tiles):
                if tiles == NT:
                    values(b, CHUNKS - 1)
                if new:
                    qk_tile(part, b, 1)
                if tiles == NT:
                    back(part, b, 3)
                if new:
                    qk_tile(part, b, 2)
                if tiles == NT:
                    pe.wait_ge(at_ready, 4 * b + 4)
                else:
                    pe.wait_ge(vcls_ready, 2)
                transpose_tiles(part, "att", b, at, tiles)
                if new:
                    qk_tile(part, b, 3)
                both(part, "att", b)
                scores = cls_scores(0 if part == "pro" else b + 1, part, b) if new else iter(())

                def one_score():
                    next(scores, None)

                for t in range(0, tiles, 2):
                    pair(part, "wo", b, t, tiles, aT, wo, one_score)
                for _ in scores:
                    pass
                if new:
                    pair(part, "v", b, 0, NT, zT, wv)
                    pair(part, "v", b, 2, NT, zT, wv)
                pe.wait_ge(z_ready, 2 * b + 5 if part == "body" else {"pro": 3, "last": 2 * B + 2}[part])
                if tiles == NT:
                    pe.wait_ge(z_late_ready, b + 1)
                transpose_tiles(part, "zt2", b, z, tiles)
                both(part, "zt2", b)
                if part == "pro":
                    pe.wait_ge(ffn_in, 64)
                ps, full = d_bank(part, ("lt",), b)
                for k in range(HT):
                    ins = T.matmul(ps[0:NE, 0:tiles * P], rw_sb[:, k, :], aT[:, k, 0:tiles * P], start=(k == 0), stop=(k == HT - 1))
                ins.then_inc(full, 1)
                w1_tile(part, b, 0)
                taken(pe, part, ("lt",), b)
                ps, full = d_bank(part, ("rt",), b)
                for t in range(tiles):
                    ins = T.transpose(ps[:, t * P:(t + 1) * P], lgT[:, t * P:(t + 1) * P], ident[:, :])
                ins.then_inc(full, 1)
                for t in range(1, tiles):
                    w1_tile(part, b, t)
                for t in range(tiles):
                    weighted(part, b, t)

            def ffn_mid(part, b, f, n, between=lambda: None):
                if f == 0 and first(b):
                    pe.wait_ge(ffn_split, 1)
                ps, full = d_bank(part, ("w2", f), b)
                width = n // 2 if f == 0 and n == S else n
                for t0 in range(0, n, width):
                    if f == 0:
                        for t in range(t0 // P, (t0 + width) // P):
                            taken(pe, tail_of(b)[0], ("tt", t), tail_of(b)[1])
                    for c in range(NC):
                        for p, (w, act) in enumerate(((w2_hi, tT_hi), (w2_hi, tT_lo), (w2_lo, tT_hi))):
                            ins = T.matmul(ps[:, t0:t0 + width], w[:, c, f * P:(f + 1) * P], act[:, c, t0:t0 + width],
                                           start=(c == 0 and p == 0), stop=(c == NC - 1 and p == 2), skip_group_check=True)
                        if c < NC - 1:
                            between()
                ins.then_inc(full, 1)
                between()

            def ffn_out(part, b, f, n, between=lambda: None):
                pe.wait_ge(g_lo_ready, NF * b + f + 1)
                if f == 0:
                    wait(pe, ot_ready, 4 * b)
                for t in range(n // P):
                    for p, (act, w) in enumerate(((g_hi, lw_hi), (g_hi, lw_lo), (g_lo, lw_hi))):
                        ins = T.matmul(bank[3 + t // 2][:, D * (t % 2):D * (t % 2 + 1)], act[:, f % 2, t * P:(t + 1) * P], w[:, f, :],
                                       start=(f == 0 and t % 2 == 0 and p == 0), stop=(f == NF - 1 and p == 2), skip_group_check=True)
                    if t < n // P - 1:
                        between()
                ins.then_inc(g_used if f < NF - 1 else lin_full, 1)
                for t in range(n // P - 1, NT):
                    between()

            def cls_scores(nb, part, b):
                taken(pe, part, ("qk", 1), b)
                if first(nb):
                    pe.wait_ge(kblk_ready, 1)
                ps, full = s_bank(S_CLS, nb)
                for qt in range(NT):
                    for ht in range(HT):
                        ins = T.matmul(ps[:, qt * NH:(qt + 1) * NH], qT[:, ht, qt * P:(qt + 1) * P], kblk[:, ht, :],
                                       start=(ht == 0), stop=(ht == HT - 1), skip_group_check=True)
                        if (qt, ht) == (NT - 1, HT - 1):
                            ins.then_inc(full, 1)
                        yield

            def max_unit(b, i):
                qt, h0, w = MAX_UNITS[i]
                n = P * (qt + 1)
                ps, full = s_bank(S_MAX + i, b)
                if i == 0:
                    pe.wait_ge(scr_r, 2 * len(Q_PART) * 16 * (b + 1))
                for j in range(w):
                    T.matmul(ps[:, j * n:(j + 1) * n], qs[0:STACK, h0 + j, qt * P:(qt + 1) * P], ks[0:STACK, h0 + j, 0:n],
                             start=True, stop=False, skip_group_check=True)
                    ins = T.matmul(ps[:, (j + 1) * n - P:(j + 1) * n], identb[:, :], maskq[:, :],
                                   start=False, stop=True, skip_group_check=True)
                ins.then_inc(full, 1)

            def turn_maxima(b):
                pe.wait_ge(mhl_ready, b + 1)
                ps, full = s_bank(S_MT, b)
                for t in range(NT):
                    ins = T.matmul(ps[STACK:P, t * P:(t + 1) * P], mhl[:, t, :], identb[:, :], start=True, stop=True)
                ins.then_inc(full, 1)

            def exp_unit(b, c, u, j, w):
                kt, n = c % NT, S - P * (c % NT)
                ps, full = s_bank(u, b)
                for i in range(w):
                    h = 4 * (c // NT) + j + i
                    T.matmul(ps[:, i * n:(i + 1) * n], ks[:, h, kt * P:(kt + 1) * P], qs[:, h, kt * P:S],
                             start=True, stop=False, skip_group_check=True)
                    ins = T.matmul(ps[:, i * n:i * n + P], identb[:, :], maskk[:, :], start=False, stop=True, skip_group_check=True)
                ins.then_inc(full, 1)

            def values(b, c):
                q, kt = c // NT, c % NT
                n = S - P * kt
                for u, _, _ in units_of(c):
                    score_taken(pe, u, b)
                if kt == 0:
                    if q < 2:
                        pe.wait_ge(out_ready, 4 * b + 1)
                    else:
                        pe.wait_ge(ot_ready, 4 * b + q - 1)
                for j in range(4):
                    ins = T.matmul(bank[3 + q % 2][32 * j:32 * j + 32, P * kt:S], va[:, kt, 4 * q + j, :], pt[:, c % 2, j, 0:n],
                                   start=(kt == 0), stop=(kt == NT - 1), skip_group_check=True)
                ins.then_inc(pv_full if kt == NT - 1 else pv_used, 1)

            def attend_group(part, b, q, new):
                c = NT * q
                pe.wait_ge(qs_max, 4 * b + q + 1)
                units = [[lambda c=c, u=u: exp_unit(b, c, *u) for u in units_of(c)] for c in range(c, c + NT)]
                tok_step = [lambda i=i: tok(part, b, q + 1, i) for i in range(4)] if new and q + 1 < NT else [nothing] * 4
                back_step = (lambda: back(part, b, q - 1)) if q else nothing
                before = (lambda: values(b, c - 1)) if q else nothing
                x_step = [lambda i=i: xt(part, b, q + 2, i) for i in range(2)] if new and q + 2 < NT else [nothing] * 2
                up = bring_up(part, b) if new and q + 1 == NT else [nothing] * 3
                for item in (
                        units[0][0], tok_step[0], units[0][1], before, units[0][2], tok_step[1], up[0], units[0][3], tok_step[2], up[1],
                        units[1][0], units[1][1], lambda: values(b, c), tok_step[3], units[1][2], back_step,
                        units[1][3], x_step[0], up[2], units[2][0], units[2][1], lambda: values(b, c + 1),
                        units[3][0], x_step[1], lambda: values(b, c + 2)):
                    item()

            def turn(part, b, n, new=True):
                units = iter(range(len(MAX_UNITS)))
                def one_unit():
                    for i in units:
                        max_unit(b, i)
                        break

                for f in range(NF - 1):
                    between = one_unit if f >= MAX_FROM else nothing
                    ffn_mid(part, b, f, n, between)
                    if f:
                        ffn_out(part, b, f - 1, n, between)
                for i in units:
                    max_unit(b, i)
                ffn_mid(part, b, NF - 1, n)
                if new:
                    xt(part, b, 0, 0)
                    xt(part, b, 0, 1)
                turn_maxima(b)
                ffn_out(part, b, NF - 2, n)
                ffn_out(part, b, NF - 1, n)
                if new:
                    for i in range(4):
                        tok(part, b, 0, i)
                    xt(part, b, 1, 0)
                    xt(part, b, 1, 1)
                for q in range(4):
                    attend_group(part, b, q, new)
                tail(part, b, new, NT)

            pe.wait_ge(consts, CONSTS)
            pe.wait_ge(identb_ready, 1)
            pe.wait_ge(tok_w, 32)
            for i in range(HT):
                ps, full = d_bank("pro", ("ws", i), 0)
                for a in range(HT):
                    ins = T.transpose(ps[:, a * P:(a + 1) * P], ws_sb[:, a, i * P:(i + 1) * P], ident[:, :])
                ins.then_inc(full, 1)
            ps, full = d_bank("pro", ("wt",), 0)
            for a in range(HT):
                ins = T.transpose(ps[0:DD, a * P:(a + 1) * P], w_sb[:, a, :], ident[:, :])
            ins.then_inc(full, 1)
            taken(pe, "pro", ("wt",), 0)
            ps, full = d_bank("pro", ("wrep",), 0)
            T.matmul(ps[:, 0:D], spread4[:, :], wT[:, :], start=True, stop=True).then_inc(full, 1)
            both("pro", "ws", 0)
            for k in range(KX):
                ps, full = d_bank("pro", ("wtok", k), 0)
                T.matmul(ps[:, 0:D], spread[:, k % 4, :], wsT[:, k // 4, :], start=True, stop=True).then_inc(full, 1)
            pe.wait_ge(z_ready, 1)
            transpose_tiles("pro", "czt", 0, z, 1)
            both("pro", "czt", 0)
            pe.wait_ge(attn_w, 64)
            ps, full = d_bank("pro", ("ck",), 0)
            for ht in range(HT):
                for k in range(HT):
                    ins = T.matmul(ps[:, ht * P:(ht + 1) * P], wq[:, k, D + ht * P:D + (ht + 1) * P], zT[:, k, 0:P],
                                   start=(k == 0), stop=(k == HT - 1))
            ins.then_inc(full, 1)
            project("pro", ("cv",), 0, lambda k: zT[:, k, 0:P], lambda k: wv[:, k, :], D)
            for i in range(KX):
                taken(pe, "pro", ("wtok", i), 0)
            for t in range(NT):
                for half in range(2):
                    xt("pro", 0, t, half)
                for i in range(4):
                    tok("pro", 0, t, i)
            for stage in bring_up("pro", 0):
                stage()
            tail("pro", 0, True, 1)
            pe.wait_ge(stack_set, 1)
            turn("body", 0, P)
            with pe.Fori(1, B - 1) as b:
                turn("body", b, S)
            turn("last", B - 1, S, False)
            for f in range(NF):
                ffn_mid("end", B, f, S)
                if f:
                    ffn_out("end", B, f - 1, S)
            ffn_out("end", B, NF - 1, S)


INPUTS = ["x", "cls_tok", "L0_tok_weight", "L0_tok_weighted_sum", "L0_attn_WQ", "L0_attn_WK", "L0_attn_WV", "L0_attn_WO",
          "L0_ffn_router_w", "L0_ffn_router_b", "L0_ffn_w1", "L0_ffn_w2", "L0_ffn_lin2_w", "L0_ffn_lin2_b"]


def kernel(**inputs):
    import numpy as np
    import concourse.bacc as bacc
    from concourse.bass_utils import run_bass_kernel_spmd

    nc = bacc.Bacc("TRN2", target_bir_lowering=False, num_devices=1)
    arrays, args = {}, []
    for name in INPUTS:
        a = np.ascontiguousarray(inputs[name])
        if name == "x":
            a = a.reshape(B, S, IN * DD)
        arrays["in_" + name] = a
        args.append(nc.dram_tensor("in_" + name, a.shape, mybir.dt.from_np(a.dtype), kind="ExternalInput").ap())
    args.append(nc.dram_tensor("out_h", (B, S + 1, D), F32, kind="ExternalOutput").ap())
    build(nc, *args)
    r = run_bass_kernel_spmd(nc, [arrays], core_ids=[0])
    return r.results[0]["out_h"]
```

```python
from contextlib import ExitStack

import concourse.bass as bass
from concourse import mybir

ALU = mybir.AluOpType
ACT = mybir.ActivationFunctionType
AX_X = mybir.AxisListType.X
F32 = mybir.dt.float32
F32R = mybir.dt.float32r
BF16 = mybir.dt.bfloat16

P = 128
B, S, IN, DD = 8, 512, 256, 4
D, NH, DK = 256, 16, 16
NE, RK, F = 8, 64, 1024
NT = S // P
KX = IN * DD // P
HT = D // P
NC = NE * RK // P
NF = F // P
CHUNKS = 4 * NT
EPS = 1e-5
MASKED = -1e30
Q_PART = (0, 0, 1, 1, 0, 2)
K_PART = (0, 1, 0, 1, 2, 0)
STACK = DK * len(Q_PART)

MAX_UNITS = [(qt, h, n) for qt, n in ((0, 4), (1, 2), (2, 1), (3, 1)) for h in range(0, NH, n)]
EXP_UNITS = [[(j, 1) for j in range(4)], [(j, 1) for j in range(4)], [(0, 2), (2, 2)], [(0, 4)]]
N_EXP = 4 * sum(len(u) for u in EXP_UNITS)
S_TAIL = [("wo", 0), ("wo", 2), ("cls",), ("lt",), ("w1", 0), ("w1", 1), ("w1", 2)]
S_CLS, S_MAX = S_TAIL.index(("cls",)), len(S_TAIL)
S_MT = S_MAX + len(MAX_UNITS)
S_EXP = S_MT + 1
S_USES = S_EXP + N_EXP
MAX_FROM = 1
SLOTS = 3
IDENT_CONSTS, SPREAD_CONSTS = 2, 7
CONSTS = 20


def tok_uses(t):
    return [("xt", t, 0), ("xt", t, 1), ("tok", t)]


UP_USES = [("zt1", 0), ("zt1", 1), ("qk", 0)]


def tail_uses(new, tiles):
    def filler(*uses):
        return list(uses) if new else []

    if tiles < NT:
        return filler(("qk", 1), ("qk", 2)) + [("att", 0), ("att", 1)] + filler(("qk", 3)) + [("wo", 0)] + filler(
            ("v", 0), ("v", 2)) + [("zt2", 0), ("zt2", 1), ("lt",), ("w1", 0), ("rt",), ("tt", 0)]
    out = filler(("qk", 1)) + [("bt", 3), ("att", 1)] + filler(("qk", 2), ("qk", 3), ("v", 0), ("v", 2)) + [("zt2", 0), ("zt2", 1)]
    return out + [("rt",), ("tt", 0), ("w1", 3)] + [("tt", t) for t in range(1, tiles)]


W2_USES = [("w2", f) for f in range(NF)]


def attention_uses(new):
    out = W2_USES[:-1] + (tok_uses(0)[0:2] if new else []) + W2_USES[-1:]
    out += tok_uses(1)[0:2] + [("tok", 0)] if new else []
    for q in range(4):
        if new and q + 1 < NT:
            out.append(("tok", q + 1))
        elif new:
            out += [("zt1", 0), ("zt1", 1)]
        if q:
            out.append(("bt", q - 1))
        if new and q + 2 < NT:
            out += tok_uses(q + 2)[0:2]
    return out + ([("qk", 0)] if new else []) + [("att", 0)]


PRO_ORDER = (
    [("ws", 0), ("ws", 1), ("wt",), ("wrep",)] + [("wtok", k) for k in range(KX)]
    + [("czt", 0), ("czt", 1), ("ck",), ("cv",)]
    + tok_uses(0)[0:2] + [u for t in range(1, NT) for u in tok_uses(t)[0:2] + [("tok", t - 1)]] + [("tok", NT - 1)] + UP_USES + tail_uses(True, 1)
)
BODY_ORDER = attention_uses(True) + tail_uses(True, NT)
LAST_ORDER = attention_uses(False) + tail_uses(False, NT)
BODY_USES = len(BODY_ORDER)
assert BODY_USES % SLOTS == 0 and S_USES % SLOTS == 0
S_MISSING = [sum(n != S_CLS and n % SLOTS == i for n in range(S_MAX)) for i in range(SLOTS)]
OFFSET = {"pro": {u: n for n, u in enumerate(PRO_ORDER)},
          "body": {u: n + len(PRO_ORDER) for n, u in enumerate(BODY_ORDER)},
          "last": {u: n + len(PRO_ORDER) for n, u in enumerate(LAST_ORDER)},
          "end": {u: n + len(PRO_ORDER) + len(LAST_ORDER) - BODY_USES for n, u in enumerate(W2_USES)}}


def wait(eng, sem, value):
    if isinstance(value, int) and value <= 0:
        return
    eng.wait_ge(sem, value)


def first(b):
    return isinstance(b, int) and b == 0


def brought_up(nb):
    return ("pro", 0) if first(nb) else ("body", nb - 1)


def tail_of(b):
    if isinstance(b, int):
        return ("pro", 0) if b == 0 else ("body", b - 1) if b < B else ("last", B - 1)
    return ("body", b - 1)


def units_of(c):
    n = S_EXP + sum(len(EXP_UNITS[k % NT]) for k in range(c))
    return [(n + i, j, w) for i, (j, w) in enumerate(EXP_UNITS[c % NT])]


class Steps:

    def __init__(self, eng, sem):
        self.eng, self.sem, self.base, self.n = eng, sem, 0, 0

    def __call__(self, ins):
        self.n += 1
        ins.then_inc(self.sem, 1)
        self.eng.wait_ge(self.sem, self.base + self.n)

    def loop(self, turn, per):
        self.start = self.n
        self.base, self.n = self.start + turn * per, 0

    def end(self, turns, per):
        assert self.n == per, (self.n, per)
        self.base, self.n = 0, self.start + turns * per


def build(nc, x, cls_tok, weight, wsum, WQ, WK, WV, WO, rw, rb, w1, w2, lw, lb, out):
    ctx = ExitStack()
    with ctx:
        def sb(name, shape, dt=F32):
            return ctx.enter_context(nc.sbuf_tensor(name, shape, dt))

        def sem(name):
            return ctx.enter_context(nc.semaphore(name))

        def overlay(*layouts):
            out = []
            for layout in layouts:
                with ExitStack() as own:
                    keep = ctx if layout is layouts[-1] else own
                    out += [keep.enter_context(nc.sbuf_tensor(name, shape, dt)) for name, shape, dt in layout]
            return out

        bank = [ctx.enter_context(nc.psum_tensor(f"bank{i}", [P, 512], F32)) for i in range(8)]
        scratch = nc.dram_tensor("qk_parts", (3, 4 * P, S), BF16, kind="Internal").ap()

        ident = sb("ident", [P, P])
        identb = sb("identb", [P, P], BF16)
        maskq = sb("maskq", [P, P], BF16)
        maskk = sb("maskk", [P, P], BF16)
        headmask = sb("headmask", [P, HT, NH])
        lower = sb("lower", [P, NE, NE], BF16)
        minus_half = sb("minus_half", [P, NT])
        select = sb("select", [P, NH], BF16)
        wtok_hi, wtok_lo = sb("wtok_hi", [P, KX, D], F32R), sb("wtok_lo", [P, KX, D], F32R)
        wq_hi, wq_lo = sb("wq_hi", [P, HT, 2 * D], F32R), sb("wq_lo", [P, HT, 2 * D], F32R)
        wv_hi, wv_lo = sb("wv_hi", [P, HT, D], F32R), sb("wv_lo", [P, HT, D], F32R)
        wo = sb("wo", [P, HT, D])
        rw_sb = sb("rw_sb", [P, HT, NE])
        rb_sb = sb("rb_sb", [P, NE])
        w1_sb = sb("w1_sb", [P, HT, NE * RK])
        w2_hi, w2_lo = sb("w2_hi", [P, NC, F], F32R), sb("w2_lo", [P, NC, F], F32R)
        lw_hi, lw_lo = sb("lw_hi", [P, NF, D], F32R), sb("lw_lo", [P, NF, D], F32R)
        bias = sb("bias", [P, D])
        vcls = sb("vcls", [P, NH, DK + 1])
        kc = sb("kc", [P, HT])
        kblk = sb("kblk", [P, HT, NH])

        z, tm, xin = overlay([("z", [P, NT, D], F32), ("tm", [P, 2, NE * RK], F32)], [("xin", [P, 2, IN * DD], F32)])
        parts, zT_hi, xT_hi, xT_lo = overlay([("parts", [P, 3, 4, S], BF16), ("zT_hi", [P, HT, S], F32R)],
                                      [("xT_hi", [P, 4, 4 * P], F32R), ("xT_lo", [P, 4, 4 * P], F32R)])
        hn = sb("hn", [P, NT, D])
        hc = sb("hc", [P, NT, D])
        x1 = sb("x1", [P, NT, D])
        zT_lo = sb("zT_lo", [P, HT, S], F32R)
        stats = sb("stats", [P, NT, 6])
        mv = sb("mv", [P, 3, NT])
        veps = sb("veps", [P, NT])
        shift = sb("shift", [P, NT])
        rstd = sb("rstd", [P, NT])
        w2_in, lw_in, qs, ks = overlay([("w2_in", [P, NC, F], F32), ("lw_in", [P, NF, D], F32)],
                                       [("qs", [P, NH, S], BF16), ("ks", [P, NH, S], BF16)])
        va = sb("va", [P, NT, NH, 2 * DK])
        cs = sb("cs", [P, NT, NH])
        top = sb("top", [P, NT, NH])
        mhl = sb("mhl", [P, NT, 2 * NH], BF16)
        msum = sb("msum", [P, NT, NH])
        mT, cmp1, cmp2 = overlay([("mT", [P, S], BF16)], [("cmp1", [P, NT, NE, NE], BF16), ("cmp2", [P, NT, NE, NE], BF16)])
        pcls = sb("pcls", [P, NT, NH])
        aT0 = sb("aT0", [P, S])
        aT1, ocls = overlay([("aT1", [P, S], F32)], [("ocls", [P, NT, NH, DK + 1], F32)])
        aT = (aT0, aT1)
        wtok, wq_in, wv_in, tT_hi, tT_lo, pt = overlay(
            [("wtok", [P, KX, D], F32), ("wq_in", [P, HT, 2 * D], F32), ("wv_in", [P, HT, D], F32)],
            [("tT_hi", [P, NC, S], F32R), ("tT_lo", [P, NC, S], F32R)], [("pt", [P, 2, 4, S], F32)])
        wsT, ws_sb, spread, wrep, spread4, w_sb, wT, g, g_hi, g_lo, ot, at, qT = overlay(
            [("wsT", [P, IN // P, D], F32), ("ws_sb", [P, HT, IN], F32),
             ("spread", [P, 4, P], F32),
             ("wrep", [P, D], F32),
             ("spread4", [DD, P], F32),
             ("w_sb", [P, HT, DD], F32), ("wT", [DD, D], F32)],
            [("g", [P, 2, S], F32), ("g_hi", [P, 2, S], F32R), ("g_lo", [P, 2, S], F32R)],
            [("ot", [P, 2, S], F32), ("at", [P, NT, D], F32), ("qT", [P, HT, S], F32)])
        num = sb("num", [P, NT, 4, DK + 1])
        rden = sb("rden", [P, NT, 4])
        lgT = sb("lgT", [P, S])
        lg = sb("lg", [P, 2, NT, NE])
        lmax = sb("lmax", [P, NT])
        lsum = sb("lsum", [P, NT])
        rank = sb("rank", [P, NT, NE])
        mw = sb("mw", [P, NT, NE])
        rest = tm

        s_full = [sem(f"s_full{i}") for i in range(SLOTS)]
        s_free = [sem(f"s_free{i}") for i in range(SLOTS)]
        d_full = [sem(f"d_full{i}") for i in range(SLOTS)]
        d_free = [sem(f"d_free{i}") for i in range(SLOTS)]
        tok_w, attn_w, cls_in, ffn_in, ffn_w, last_bias = (
            sem(n) for n in ("tok_w", "attn_w", "cls_in", "ffn_in", "ffn_w", "last_bias"))
        x_full = [sem(f"x_full{i}") for i in range(2)]
        consts = sem("consts")
        dve_step = sem("dve_step")
        identb_ready, stack_set, va_set = sem("identb_ready"), sem("stack_set"), sem("va_set")
        kblk_ready, vcls_ready = sem("kblk_ready"), sem("vcls_ready")
        hc_ready = sem("hc_ready")
        var_ready, rstd_ready = sem("var_ready"), sem("rstd_ready")
        z_ready = sem("z_ready")
        shift_ready, z_late_ready = sem("shift_ready"), sem("z_late_ready")
        first_ready, second_ready, third_ready = sem("first_ready"), sem("second_ready"), sem("third_ready")
        scr_w = [sem(f"scr_w{p}") for p in range(3)]
        scr_r = sem("scr_r")
        mhl_ready, cs_ready, pcls_ready, ocls_ready = (
            sem(n) for n in ("mhl_ready", "cs_ready", "pcls_ready", "ocls_ready"))
        qs_max = sem("qs_max")
        pv_used = sem("pv_used")
        pv_full, ot_ready = sem("pv_full"), sem("ot_ready")
        num_ready, at_ready = sem("num_ready"), sem("at_ready")
        bias_added = sem("bias_added")
        wq_hi_ready, wv_hi_ready, attn_split = sem("wq_hi_ready"), sem("wv_hi_ready"), sem("attn_split")
        wtok_ready, wtok_hi_ready = sem("wtok_ready"), sem("wtok_hi_ready")
        w2_hi_ready, lw_hi_ready, ffn_split = sem("w2_hi_ready"), sem("lw_hi_ready"), sem("ffn_split")
        tT_hi_ready = sem("tT_hi_ready")
        g_hi_ready, g_lo_ready = sem("g_hi_ready"), sem("g_lo_ready")
        lexp = sem("lexp")
        g_used = sem("g_used")
        lin_full, out_ready, out_stored = sem("lin_full"), sem("out_ready"), sem("out_stored")

        def d_at(part, name, b):
            if part in ("body", "last") and name in S_TAIL:
                return s_at(S_TAIL.index(name), b + 1)
            n = OFFSET[part][name]
            i, k = n % SLOTS, n // SLOTS
            return bank[5 + i], d_full[i], d_free[i], k if part == "pro" else b * (BODY_USES // SLOTS) + k

        def s_at(n, b):
            i, k = n % SLOTS, n // SLOTS
            if not first(b) or n >= S_MAX:
                k -= S_MISSING[i]
            if isinstance(b, int) and b == B and n > S_CLS and i == S_CLS % SLOTS:
                k -= 1
            return bank[i], s_full[i], s_free[i], b * (S_USES // SLOTS) + k

        def written(eng, part, name, b):
            ps, full, free, k = d_at(part, name, b)
            eng.wait_ge(full, k + 1)
            return ps, free

        def taken(eng, part, name, b):
            ps, full, free, k = d_at(part, name, b)
            eng.wait_ge(free, k + 1)

        def scored(eng, n, b):
            ps, full, free, k = s_at(n, b)
            eng.wait_ge(full, k + 1)
            return ps, free

        def score_taken(eng, n, b):
            ps, full, free, k = s_at(n, b)
            eng.wait_ge(free, k + 1)

        block = ctx.enter_context(nc.Block())

        @block.sync
        def _(sp):
            def load_x(b, t):
                if t >= 2:
                    written(sp, brought_up(b)[0], ("xt", t - 2, 1), brought_up(b)[1])
                elif not first(b):
                    part, turn_ = tail_of(b - 1)
                    written(sp, part, ("tt", 0 if part == "pro" else NT - 1), turn_)
                sp.dma_start(xin[:, t % 2, :], x[b, t * P:(t + 1) * P, :]).then_inc(x_full[t % 2], 16)

            def stack(b):
                wait(sp, scr_r, 2 * len(Q_PART) * 16 * b)
                for p, ready in enumerate((first_ready, second_ready, third_ready)):
                    sp.wait_ge(ready, 4 * b + 4)
                    sp.dma_start(scratch[p].rearrange("(a r) t -> r a t", r=P), parts[:, p, :, :]).then_inc(scr_w[p], 16)
                if first(b):
                    sp.wait_ge(ffn_split, 1)
                else:
                    scored(sp, S_USES - 1, b - 1)
                for p in range(3):
                    sp.wait_ge(scr_w[p], 16 * b + 16)
                    for j in range(len(Q_PART)):
                        rows = slice(DK * j, DK * j + DK)
                        if Q_PART[j] == p:
                            sp.dma_start(qs[rows, :, :], scratch[p][0:2 * P].rearrange("(h d) t -> d h t", d=DK)).then_inc(scr_r, 16)
                        if K_PART[j] == p:
                            sp.dma_start(ks[rows, :, :], scratch[p][2 * P:4 * P].rearrange("(h d) t -> d h t", d=DK)).then_inc(scr_r, 16)

            def store(b):
                sp.wait_ge(out_ready, 4 * b + 5)
                sp.dma_start(out[b, 1:, :].rearrange("(t p) d -> p t d", p=P), x1[:, :, :]).then_inc(out_stored, 16)

            sp.dma_start(ws_sb[:, :, :], wsum.rearrange("(a p) i -> p a i", p=P)).then_inc(tok_w, 16)
            sp.dma_start(w_sb[:, :, :], weight.rearrange("(a p) d -> p a d", p=P)).then_inc(tok_w, 16)
            sp.dma_start(hc[:, 0, :], cls_tok[0].broadcast_to([P, D])).then_inc(cls_in, 16)
            load_x(0, 0)
            load_x(0, 1)
            sp.dma_start(wq_in[:, :, 0:D], WQ.rearrange("(k p) n -> p k n", p=P)).then_inc(attn_w, 16)
            sp.dma_start(wq_in[:, :, D:2 * D], WK.rearrange("(k p) n -> p k n", p=P)).then_inc(attn_w, 16)
            sp.dma_start(wv_in[:, :, :], WV.rearrange("(k p) n -> p k n", p=P)).then_inc(attn_w, 16)
            sp.dma_start(wo[:, :, :], WO.rearrange("(k p) n -> p k n", p=P)).then_inc(attn_w, 16)
            sp.dma_start(rw_sb[:, :, :], rw.rearrange("(k p) n -> p k n", p=P)).then_inc(ffn_in, 16)
            sp.dma_start(rb_sb[:, :], rb.rearrange("(a n) -> a n", a=1).broadcast_to([P, NE])).then_inc(ffn_in, 16)
            for k in range(HT):
                sp.dma_start(w1_sb[:, k, :].rearrange("p (e r) -> p e r", r=RK),
                             w1[:, k * P:(k + 1) * P, :].rearrange("e p r -> p e r")).then_inc(ffn_in, 16)
            sp.dma_start(bias[:, :], lb.rearrange("(a n) -> a n", a=1).broadcast_to([P, D])).then_inc(last_bias, 16)
            load_x(0, 2)
            load_x(0, 3)
            sp.dma_start(w2_in[:, :, :], w2.rearrange("e r f -> (e r) f").rearrange("(c p) f -> p c f", p=P)).then_inc(ffn_w, 16)
            sp.dma_start(lw_in[:, :, :], lw.rearrange("(c p) n -> p c n", p=P)).then_inc(ffn_w, 16)
            stack(0)

            def turn(b, new=True):
                if new:
                    load_x(b + 1, 0)
                    load_x(b + 1, 1)
                if first(b):
                    sp.wait_ge(out_ready, 1)
                    sp.dma_start(out[:, 0, :], x1[0:B, 0, :]).then_inc(out_stored, 16)
                else:
                    store(b - 1)
                if new:
                    load_x(b + 1, 2)
                    load_x(b + 1, 3)
                    stack(b + 1)

            turn(0)
            with sp.Fori(1, B - 1) as b:
                turn(b)
            turn(B - 1, False)
            store(B - 1)
            sp.wait_ge(out_stored, 16 * (B + 1))

        @block.gpsimd
        def _(pool):
            G = nc.gpsimd
            step = Steps(pool, consts)
            step(G.memset(ident[:, :], 0.0))
            step(G.affine_select(out=ident[:, :], in_=ident[:, :], compare_op=ALU.not_equal, fill=1.0, base=0,
                            pattern=[[-1, P]], channel_multiplier=1))
            step(G.memset(spread[:, :, :], 1.0))
            step(G.memset(spread4[:, :], 0.0))
            step(G.affine_select(out=spread[:, :, :], in_=spread[:, :, :], compare_op=ALU.is_ge, fill=0.0, base=0,
                                 pattern=[[P, 4], [1, P]], channel_multiplier=-4))
            step(G.affine_select(out=spread[:, :, :], in_=spread[:, :, :], compare_op=ALU.is_ge, fill=0.0, base=3,
                            pattern=[[-P, 4], [-1, P]], channel_multiplier=4))
            by_d = spread4[:, :].rearrange("d (i k) -> d i k", k=DD)
            step(G.affine_select(out=by_d, in_=by_d, compare_op=ALU.not_equal, fill=1.0, base=0,
                            pattern=[[0, P // DD], [-1, DD]], channel_multiplier=1))
            assert step.n == SPREAD_CONSTS
            step(G.memset(minus_half[:, :], -0.5))
            step(G.memset(headmask[:, :, :], 1.0))
            step(G.affine_select(out=headmask[:, :, :], in_=headmask[:, :, :], compare_op=ALU.is_ge, fill=0.0, base=0,
                                 pattern=[[P, HT], [-DK, NH]], channel_multiplier=1))
            step(G.affine_select(out=headmask[:, :, :], in_=headmask[:, :, :], compare_op=ALU.is_ge, fill=0.0, base=DK - 1,
                            pattern=[[-P, HT], [DK, NH]], channel_multiplier=-1))
            step(G.memset(maskq[:, :], 0.0))
            step(G.memset(maskk[:, :], 0.0))
            step(G.affine_select(out=maskq[:, :], in_=maskq[:, :], compare_op=ALU.is_ge, fill=MASKED, base=0,
                            pattern=[[-1, P]], channel_multiplier=1))
            step(G.affine_select(out=maskk[:, :], in_=maskk[:, :], compare_op=ALU.is_ge, fill=MASKED, base=0,
                            pattern=[[1, P]], channel_multiplier=-1))
            step(G.memset(lower[:, :, :], 1.0))
            step(G.affine_select(out=lower[:, :, :], in_=lower[:, :, :], compare_op=ALU.is_gt, fill=0.0, base=0,
                            pattern=[[1, NE], [-1, NE]], channel_multiplier=0))
            sel = select[STACK:P, :]
            step(G.memset(sel, 0.0))
            step(G.affine_select(out=sel, in_=sel, compare_op=ALU.not_equal, fill=-1.0, base=0,
                                 pattern=[[-1, NH]], channel_multiplier=1))
            step(G.affine_select(out=sel, in_=sel, compare_op=ALU.not_equal, fill=-1.0, base=-NH,
                            pattern=[[-1, NH]], channel_multiplier=1))

            assert step.n == CONSTS

            def rsqrt(n, tiles):
                pool.wait_ge(var_ready, n + 1)
                G.tensor_tensor(rstd[:, 0:tiles], veps[:, 0:tiles], minus_half[:, 0:tiles], ALU.pow).then_inc(rstd_ready, 1)

            def third_parts(b, tiles):
                for j in tiles:
                    pool.wait_ge(second_ready, 4 * b + j + 1)
                    if j == 0:
                        wait(pool, scr_w[2], 16 * b)
                    G.tensor_tensor(parts[:, 2, j, :], rest[:, j % 2, :], parts[:, 1, j, :], ALU.subtract).then_inc(third_ready, 1)

            def cls_values(b):
                pool.wait_ge(pcls_ready, b + 1)
                if first(b):
                    pool.wait_ge(vcls_ready, 2)
                wait(pool, num_ready, 4 * b)
                G.tensor_tensor(ocls[:, :, :, :],
                                pcls[:, :, :].rearrange("p t (h a) -> p t h a", a=1).broadcast_to([P, NT, NH, DK + 1]),
                                vcls[:, :, :].rearrange("p (a h) d -> p a h d", a=1).broadcast_to([P, NT, NH, DK + 1]),
                                ALU.mult).then_inc(ocls_ready, 1)

            def add_bias(part, b, j, tiles):
                pool.wait_ge(z_ready, 2 * b + 5 if part == "body" else {"pro": 3, "last": 2 * B + 2}[part])
                if tiles == NT:
                    pool.wait_ge(z_late_ready, b + 1)
                if first(j):
                    pool.wait_ge(last_bias, 16)
                G.tensor_tensor(x1[:, 0:tiles, :], x1[:, 0:tiles, :],
                                bias[:, :].rearrange("p (a d) -> p a d", a=1).broadcast_to([P, tiles, D]),
                                ALU.add).then_inc(bias_added, 1)

            rsqrt(0, 1)
            rsqrt(1, NT)
            third_parts(0, (0, 1))
            rsqrt(2, 1)
            third_parts(0, (2, 3))
            add_bias("pro", 0, 0, 1)
            pool.wait_ge(ffn_split, 1)
            pool.wait_ge(bias_added, 1)
            G.tensor_copy(ks[STACK:P, :, :], select[STACK:P, :].rearrange("p (h a) -> p h a", a=1).broadcast_to([P - STACK, NH, S])).then_inc(stack_set, 1)
            pool.wait_ge(stack_set, 1)

            def turn(part, b, new=True):
                cls_values(b)
                if new:
                    rsqrt(2 * b + 3, NT)
                    third_parts(b + 1, (0, 1))
                rsqrt(2 * b + 4 if new else 2 * b + 3, NT)
                if new:
                    third_parts(b + 1, (2, 3))
                add_bias(part, b, b + 1, NT)

            turn("body", 0)
            with pool.Fori(1, B - 1) as b:
                turn("body", b)
            turn("last", B - 1, False)

        @block.scalar
        def _(act):
            A = nc.scalar

            def copy(part, name, b, dst, src):
                ps, free = written(act, part, name, b)
                A.activation(dst, src(ps), ACT.Copy).then_inc(free, 1)

            def first_part(part, b, nb, i):
                if i == 0:
                    wait(act, scr_w[0], 16 * nb)
                ps, free = written(act, part, ("qk", i), b)
                if i < HT:
                    A.activation(qT[:, i, :], ps[:, :], ACT.Copy)
                A.activation(parts[:, 0, i, :], ps[:, :], ACT.Copy).then_inc(first_ready, 1)

            def second_part(part, b, nb, i):
                if i == 0:
                    wait(act, scr_w[1], 16 * nb)
                taken(act, part, ("qk", i), b)
                A.activation(parts[:, 1, i, :], rest[:, i % 2, :], ACT.Copy).then_inc(second_ready, 1)

            def v_tiles(part, b, t):
                copy(part, ("v", t), b, va[:, t:t + 2, :, 0:DK], lambda ps: ps[:, :].rearrange("p (t h d) -> p t h d", t=2, d=DK))

            def tT_tile(part, b, t):
                ps, free = written(act, part, ("tt", t), b)
                A.activation(tT_hi[:, :, t * P:(t + 1) * P], ps[:, :].rearrange("p (c n) -> p c n", c=NC),
                             ACT.Copy).then_inc(tT_hi_ready, 1)

            def tail(part, b, nb, new, tiles):
                if part != "pro":
                    copy(part, ("att", 0), b, aT[0][:, :], lambda ps: ps[:, :])
                if new:
                    first_part(part, b, nb, 0)
                    first_part(part, b, nb, 1)
                    second_part(part, b, nb, 0)
                if part != "pro":
                    copy(part, ("att", 1), b, aT[1][:, :], lambda ps: ps[:, :])
                if new:
                    second_part(part, b, nb, 1)
                    first_part(part, b, nb, 2)
                if part == "pro":
                    for ht in range(HT):
                        copy(part, ("att", ht), b, aT[ht][:, 0:P], lambda ps: ps[:, 0:P])
                if new:
                    second_part(part, b, nb, 2)
                    first_part(part, b, nb, 3)
                    if part == "pro":
                        act.wait_ge(va_set, 1)
                    v_tiles(part, b, 0)
                if tiles == NT:
                    act.wait_ge(shift_ready, b + 1)
                    for t in (2, 3):
                        ins = A.activation(z[:, t, :], x1[:, t, :], ACT.Identity, scale=rstd[:, t:t + 1], bias=shift[:, t:t + 1])
                    ins.then_inc(z_late_ready, 1)
                copy(part, ("zt2", 0), b, aT[0][:, 0:tiles * P], lambda ps: ps[:, 0:tiles * P])
                if new:
                    v_tiles(part, b, 2)
                    second_part(part, b, nb, 3)
                copy(part, ("lt",), b, lgT[0:NE, 0:tiles * P], lambda ps: ps[0:NE, 0:tiles * P])
                taken(act, part, ("rt",), b)
                A.activation(lg[:, 1, 0:tiles, :], lg[:, 1, 0:tiles, :], ACT.Exp).then_inc(lexp, 1)
                for t in range(tiles):
                    tT_tile(part, b, t)

            def gelus(part, b, n):
                for f in range(NF):
                    if f < 2:
                        wait(act, lin_full, b)
                    else:
                        act.wait_ge(g_used, (NF - 1) * b + f - 1)
                    ps, free = written(act, part, ("w2", f), b)
                    A.activation(g[:, f % 2, 0:n], ps[:, 0:n], ACT.Gelu).then_inc(free, 1)
                    taken(act, part, ("w2", f), b)
                    A.activation(g_hi[:, f % 2, 0:n], g[:, f % 2, 0:n], ACT.Copy).then_inc(g_hi_ready, 1)

            def exps(b, c):
                q, kt = (c - 2) // NT, (c - 2) % NT
                if kt == NT - 1:
                    wait(act, pv_full, 4 * b + q + 1)
                else:
                    wait(act, pv_used, (CHUNKS - 4) * b + (NT - 1) * q + kt + 1)
                n = S - P * (c % NT)
                for u, j, w in units_of(c):
                    ps, free = scored(act, u, b)
                    A.activation(pt[:, c % 2, j:j + w, 0:n], ps[:, 0:w * n].rearrange("p (h n) -> p h n", h=w),
                                 ACT.Exp, scale=DK ** -0.5).then_inc(free, 1)

            def copy_h(b):
                part, turn_ = tail_of(b)
                taken(act, part, ("wo", 0 if first(b) else NT - 2), turn_)
                A.activation(hc[:, :, :], hn[:, :, :], ACT.Copy).then_inc(hc_ready, 1)

            def turn(part, b, n, new=True):
                copy_h(b)
                gelus(part, b, n)
                act.wait_ge(cs_ready, b + 1)
                wait(act, ocls_ready, b)
                A.activation(pcls[:, :, :], cs[:, :, :], ACT.Exp, scale=DK ** -0.5).then_inc(pcls_ready, 1)
                for c in range(CHUNKS):
                    exps(b, c)
                tail(part, b, b + 1, new, NT)

            for i in range(HT):
                copy("pro", ("ws", i), 0, wsT[:, i, :], lambda ps: ps[:, 0:D])
            copy("pro", ("wt",), 0, wT[:, :], lambda ps: ps[0:DD, 0:D])
            copy("pro", ("wrep",), 0, wrep[:, :], lambda ps: ps[:, 0:D])
            for k in range(KX):
                act.wait_ge(wtok_ready, k + 1)
                A.activation(wtok_hi[:, k, :], wtok[:, k, :], ACT.Copy).then_inc(wtok_hi_ready, 1)
            for ht in range(HT):
                copy("pro", ("czt", ht), 0, aT[ht][:, 0:P], lambda ps: ps[:, 0:P])
            copy("pro", ("ck",), 0, kc[:, :], lambda ps: ps[:, 0:HT * P].rearrange("p (a n) -> p a n", n=P)[:, :, 0])
            copy("pro", ("cv",), 0, vcls[:, :, 0:DK], lambda ps: ps[:, 0:D].rearrange("p (h d) -> p h d", d=DK))
            act.wait_ge(attn_w, 64)
            A.activation(wq_hi[:, :, :], wq_in[:, :, :], ACT.Copy).then_inc(wq_hi_ready, 1)
            A.activation(wv_hi[:, :, :], wv_in[:, :, :], ACT.Copy).then_inc(wv_hi_ready, 1)
            act.wait_ge(ffn_w, 32)
            for c in range(NC):
                A.activation(w2_hi[:, c, :], w2_in[:, c, :], ACT.Copy).then_inc(w2_hi_ready, 1)
            A.activation(lw_hi[:, :, :], lw_in[:, :, :], ACT.Copy).then_inc(lw_hi_ready, 1)
            tail("pro", 0, 0, True, 1)
            turn("body", 0, P)
            with act.Fori(1, B - 1) as b:
                turn("body", b, S)
            turn("last", B - 1, S, False)
            gelus("end", B, S)

        @block.vector
        def _(dve):
            V = nc.vector
            step = Steps(dve, dve_step)

            def layer_norm(n, src, tiles, shared=False, dst=z, meanwhile=lambda: None):
                even, odd = stats[:, 0:tiles, 0:3], stats[:, 0:tiles, 3:6]
                mean, dif, var = mv[:, 0, 0:tiles], mv[:, 1, 0:tiles], mv[:, 2, 0:tiles]
                V.tensor_tensor(mean, even[:, :, 1], odd[:, :, 1], ALU.add)
                V.tensor_tensor(dif, even[:, :, 1], odd[:, :, 1], ALU.subtract)
                step(V.tensor_tensor(var, even[:, :, 2], odd[:, :, 2], ALU.add))
                V.tensor_scalar(mean, mean, 0.5, None, ALU.mult)
                V.tensor_scalar(var, var, 1.0 / D, EPS, ALU.mult, ALU.add)
                step(V.scalar_tensor_tensor(out=dif, in0=dif, scalar=0.25, in1=dif, op0=ALU.mult, op1=ALU.mult))
                V.tensor_tensor(veps[:, 0:tiles], var, dif, ALU.add).then_inc(var_ready, 1)
                meanwhile()
                dve.wait_ge(rstd_ready, n + 1)
                if shared:
                    V.scalar_tensor_tensor(out=shift[:, :], in0=mean, scalar=-1.0, in1=rstd[:, :], op0=ALU.mult,
                                           op1=ALU.mult).then_inc(shift_ready, 1)
                for t in range(2 if shared else tiles):
                    ins = V.tensor_scalar(dst[:, t, :], src[:, t, :], mv[:, 0, t:t + 1], rstd[:, t:t + 1], ALU.subtract, ALU.mult)
                ins.then_inc(z_ready, 1)

            def copy(part, name, b, dst, src):
                ps, free = written(dve, part, name, b)
                V.tensor_copy(dst, src(ps)).then_inc(free, 1)

            def split_copy(part, name, b, high, low):
                ps, free = written(dve, part, name, b)
                step(V.tensor_copy(high, ps[:, :]))
                V.tensor_tensor(low, ps[:, :], high.bitcast(F32), ALU.subtract).then_inc(free, 1)

            def take_x(part, b, t, half):
                if part != "pro" and (t, half) == (0, 0):
                    for stored in scr_w:
                        dve.wait_ge(stored, 16 * b + 16)
                i = 2 * (t % 2) + half
                split_copy(part, ("xt", t, half), b, xT_hi[:, i, :], xT_lo[:, i, :])

            def take_h(part, b, t):
                if part != "pro" and t == 0:
                    dve.wait_ge(hc_ready, b + 1)
                copy(part, ("tok", t), b, hn[:, t, :], lambda ps: ps[:, 0:D])
                taken(dve, part, ("tok", t), b)
                step(V.bn_stats(stats[:, t, :], hn[:, t, :]))

            def split(part, b, nb, j):
                dve.wait_ge(first_ready, 4 * nb + j + 1)
                wait(dve, third_ready, 4 * nb + j - 1)
                ps, free = written(dve, part, ("qk", j), b)
                V.tensor_tensor(rest[:, j % 2, :], ps[:, :], parts[:, 0, j, :], ALU.subtract).then_inc(free, 1)

            def take_z(part, b):
                for ht in range(HT):
                    split_copy(part, ("zt1", ht), b, zT_hi[:, ht, :], zT_lo[:, ht, :])

            def take_group(b, q):
                dve.wait_ge(pv_full, 4 * b + q + 1)
                V.tensor_copy(ot[:, q % 2, :], bank[3 + q % 2][:, :]).then_inc(ot_ready, 1)

            def normalise(part, b, q):
                if q == 0:
                    dve.wait_ge(ocls_ready, b + 1)
                ps, free = written(dve, part, ("bt", q), b)
                group = ps[:, :].rearrange("p (t h d) -> p t h d", t=NT, h=4)
                wait(dve, at_ready, 4 * b + q)
                V.tensor_tensor(num[:, :, :, :], group[:, :, :, 0:DK + 1], ocls[:, :, 4 * q:4 * q + 4, :], ALU.add).then_inc(free, 1)
                taken(dve, part, ("bt", q), b)
                V.reciprocal(rden[:, :, :], num[:, :, :, DK]).then_inc(num_ready, 1)
                dve.wait_ge(num_ready, 4 * b + q + 1)
                o = at[:, :, 4 * DK * q:4 * DK * (q + 1)].rearrange("p t (h d) -> p t h d", h=4)
                r = rden[:, :, :].rearrange("p t (h a) -> p t h a", a=1).broadcast_to([P, NT, 4, DK])
                V.tensor_tensor(o, num[:, :, :, 0:DK], r, ALU.mult).then_inc(at_ready, 1)

            def router(part, b, j, tiles):
                ps, free = written(dve, part, ("rt",), b)
                logits = ps[:, 0:tiles * P].rearrange("p (t e) -> p t e", e=P)[:, :, 0:NE]
                own_lg, less_max = lg[:, 0, 0:tiles, :], lg[:, 1, 0:tiles, :]

                def over_experts(a):
                    return a[:, 0:tiles].rearrange("p (t a) -> p t a", a=1).broadcast_to([P, tiles, NE])

                bias_lg = rb_sb[:, :].rearrange("p (a e) -> p a e", a=1).broadcast_to([P, tiles, NE])
                if first(j):
                    dve.wait_ge(ffn_in, 64)
                step(V.tensor_tensor(own_lg, logits, bias_lg, ALU.add))
                step(V.tensor_reduce(lmax[:, 0:tiles], own_lg, AX_X, ALU.max))
                V.tensor_tensor(less_max, own_lg, over_experts(lmax), ALU.subtract).then_inc(free, 1)
                shape = [P, tiles, NE, NE]
                other = own_lg.rearrange("p t (a j) -> p t a j", a=1).broadcast_to(shape)
                own = own_lg.rearrange("p t (e a) -> p t e a", a=1).broadcast_to(shape)
                low = lower[:, :, :].rearrange("p (a e) j -> p a e j", a=1).broadcast_to(shape)
                gt, eq = cmp1[:, 0:tiles, :, :], cmp2[:, 0:tiles, :, :]
                V.tensor_tensor(gt, other, own, ALU.is_gt)
                step(V.tensor_tensor(eq, other, own, ALU.is_equal))
                step(V.tensor_tensor(eq, eq, low, ALU.mult))
                step(V.tensor_tensor(gt, gt, eq, ALU.add))
                dve.wait_ge(lexp, j + 1)
                V.tensor_reduce(rank[:, 0:tiles, :], gt, AX_X, ALU.add)
                step(V.tensor_reduce(lsum[:, 0:tiles], less_max, AX_X, ALU.add))
                V.reciprocal(lsum[:, 0:tiles], lsum[:, 0:tiles])
                step(V.scalar_tensor_tensor(out=mw[:, 0:tiles, :], in0=rank[:, 0:tiles, :], scalar=2.0,
                                            in1=less_max, op0=ALU.is_lt, op1=ALU.mult))
                step(V.tensor_tensor(mw[:, 0:tiles, :], mw[:, 0:tiles, :], over_experts(lsum), ALU.mult))

            def tT_rest(part, b, j, t):
                dve.wait_ge(tT_hi_ready, 1 if part == "pro" else 4 * j - 2 + t)
                ps, free = written(dve, part, ("tt", t), b)
                cols = slice(t * P, (t + 1) * P)
                V.tensor_tensor(tT_lo[:, :, cols], ps[:, :].rearrange("p (c n) -> p c n", c=NC), tT_hi[:, :, cols].bitcast(F32),
                                ALU.subtract).then_inc(free, 1)

            def g_rest(b, f, n):
                dve.wait_ge(g_hi_ready, NF * b + f + 1)
                V.tensor_tensor(g_lo[:, f % 2, 0:n], g[:, f % 2, 0:n], g_hi[:, f % 2, 0:n].bitcast(F32), ALU.subtract).then_inc(g_lo_ready, 1)

            def take_cls(nb):
                wait(dve, pcls_ready, nb)
                ps, free = scored(dve, S_CLS, nb)
                V.tensor_copy(cs[:, :, :], ps[:, 0:NT * NH].rearrange("p (t h) -> p t h", h=NH)).then_inc(free, 1)

            def w2_rest(c):
                dve.wait_ge(w2_hi_ready, c + 1)
                V.tensor_tensor(w2_lo[:, c, :], w2_in[:, c, :], w2_hi[:, c, :].bitcast(F32), ALU.subtract)

            def lw_rest():
                dve.wait_ge(lw_hi_ready, 1)
                V.tensor_tensor(lw_lo[:, :, :], lw_in[:, :, :], lw_hi[:, :, :].bitcast(F32), ALU.subtract).then_inc(ffn_split, 1)

            def tail(part, b, j, new, tiles):
                if tiles == NT:
                    take_group(b, 3)
                if new:
                    split(part, b, j, 0)
                if tiles == NT:
                    normalise(part, b, 3)
                if new:
                    split(part, b, j, 1)
                if part == "pro":
                    w2_rest(3)
                if new:
                    split(part, b, j, 2)
                if part == "pro":
                    split(part, b, j, 3)
                    lw_rest()
                for t in range(0, tiles, 2):
                    w = min(2, tiles)
                    if part != "pro" and t == 0:
                        dve.wait_ge(hc_ready, b + 1)
                        dve.wait_ge(out_stored, 16 * j)
                    ps, free = written(dve, part, ("wo", t), b)
                    V.tensor_tensor(x1[:, t:t + w, :], ps[:, 0:w * D].rearrange("p (t d) -> p t d", t=w), hc[:, t:t + w, :],
                                    ALU.add).then_inc(free, 1)
                    taken(dve, part, ("wo", t), b)
                    for i in range(t, t + w):
                        ins = V.bn_stats(stats[:, i, :], x1[:, i, :])
                    step(ins)
                n = {"pro": 2, "last": 2 * B + 1}[part] if part != "body" else 2 * b + 4
                layer_norm(n, x1, tiles, tiles == NT, meanwhile=lambda: split(part, b, j, 3) if part == "body" else None)
                copy(part, ("zt2", 1), b, aT[1][:, 0:tiles * P], lambda ps: ps[:, 0:tiles * P])
                if new:
                    take_cls(j)
                    dve.wait_ge(third_ready, 4 * j + 4)
                router(part, b, j, tiles)
                for t in range(tiles):
                    if t >= 2:
                        written(dve, part, ("tt", t - 2), b)
                    ps, free = written(dve, part, ("w1", t), b)
                    V.tensor_tensor(tm[:, t % 2, :].rearrange("p (e r) -> p e r", r=RK), ps[:, :].rearrange("p (e r) -> p e r", r=RK),
                                    mw[:, t, :].rearrange("p (e a) -> p e a", a=1).broadcast_to([P, NE, RK]), ALU.mult).then_inc(free, 1)
                    if t >= 2:
                        tT_rest(part, b, j, t - 2)
                for t in range(max(tiles - 2, 0), tiles):
                    tT_rest(part, b, j, t)

            def finish(b, tiles):
                dve.wait_ge(lin_full, b + 1)
                dve.wait_ge(bias_added, b + 1)
                for t in range(tiles):
                    V.tensor_tensor(x1[:, t, :], bank[3 + t // 2][:, D * (t % 2):D * (t % 2 + 1)], x1[:, t, :], ALU.add).then_inc(out_ready, 1)

            def maxima(b, tiles):
                for i, (qt, h, w) in enumerate(MAX_UNITS):
                    if i % 8 == 0:
                        g_rest(b, i // 8, tiles * P)
                    n = P * (qt + 1)
                    ps, free = scored(dve, S_MAX + i, b)
                    V.tensor_reduce(top[:, qt, h:h + w], ps[:, 0:w * n].rearrange("p (h n) -> p h n", h=w), AX_X, ALU.max).then_inc(free, 1)
                for u in (S_CLS, S_MT - 3, S_MT - 2, S_MT - 1):
                    score_taken(dve, u, b)
                hi, lo = mhl[:, :, 0:NH], mhl[:, :, NH:2 * NH]
                step(V.tensor_tensor(top[:, :, :], top[:, :, :], cs[:, :, :], ALU.max))
                step(V.tensor_copy(hi, top[:, :, :]))
                V.tensor_tensor(lo, top[:, :, :], hi, ALU.subtract).then_inc(mhl_ready, 1)
                dve.wait_ge(mhl_ready, b + 1)
                step(V.tensor_tensor(msum[:, :, :], hi, lo, ALU.add))
                V.tensor_tensor(cs[:, :, :], cs[:, :, :], msum[:, :, :], ALU.subtract).then_inc(cs_ready, 1)

            def max_rows(b):
                ps, free = scored(dve, S_MT, b)
                V.tensor_copy(mT[STACK:P, :], ps[STACK:P, :]).then_inc(free, 1)
                score_taken(dve, S_MT, b)

            def spread_rows(q):
                V.tensor_copy(qs[STACK:P, 4 * q:4 * q + 4, :],
                              mT[STACK:P, :].rearrange("p (a t) -> p a t", a=1).broadcast_to([P - STACK, 4, S])).then_inc(qs_max, 1)

            def turn(part, b, tiles, new=True):
                maxima(b, tiles)
                if new:
                    take_x(part, b, 0, 0)
                g_rest(b, NF - 2, tiles * P)
                if new:
                    take_x(part, b, 0, 1)
                max_rows(b)
                g_rest(b, NF - 1, tiles * P)
                spread_rows(0)
                if new:
                    take_x(part, b, 1, 0)
                    take_x(part, b, 1, 1)
                spread_rows(1)
                finish(b, tiles)
                spread_rows(2)
                spread_rows(3)
                if new:
                    take_h(part, b, 0)
                for q in range(4):
                    if q:
                        take_group(b, q - 1)
                    if new and q + 1 < NT:
                        take_h(part, b, q + 1)
                    if new and q + 2 == NT:
                        layer_norm(2 * b + 3, hn, NT)
                    if new and q + 1 == NT:
                        take_z(part, b)
                    if q:
                        normalise(part, b, q - 1)
                    if new and q + 2 < NT:
                        take_x(part, b, q + 2, 0)
                        take_x(part, b, q + 2, 1)
                tail(part, b, b + 1, new, NT)

            dve.wait_ge(consts, IDENT_CONSTS)
            V.tensor_copy(identb[:, :], ident[:, :]).then_inc(identb_ready, 1)
            dve.wait_ge(cls_in, 16)
            step(V.bn_stats(stats[:, 0, :], hc[:, 0, :]))
            layer_norm(0, hc, 1, dst=x1)
            V.memset(lgT[:, :], 0.0)
            V.memset(va[:, :, :, DK:DK + 1], 1.0)
            V.memset(va[:, :, :, DK + 1:2 * DK], 0.0).then_inc(va_set, 1)
            V.memset(vcls[:, :, DK:DK + 1], 1.0).then_inc(vcls_ready, 1)
            taken(dve, "pro", ("wrep",), 0)

            for k in range(KX):
                ps, free = written(dve, "pro", ("wtok", k), 0)
                V.tensor_tensor(wtok[:, k, :], ps[:, 0:D], wrep[:, :], ALU.mult).then_inc(wtok_ready, 1)
                dve.wait_ge(wtok_hi_ready, k + 1)
                V.tensor_tensor(wtok_lo[:, k, :], wtok[:, k, :], wtok_hi[:, k, :].bitcast(F32), ALU.subtract).then_inc(free, 1)
            dve.wait_ge(consts, CONSTS)
            taken(dve, "pro", ("ck",), 0)
            for ht in range(HT):
                ins = V.tensor_scalar(kblk[:, ht, :], headmask[:, ht, :], kc[:, ht:ht + 1], None, ALU.mult)
            ins.then_inc(kblk_ready, 1)
            taken(dve, "pro", ("cv",), 0)
            V.tensor_copy(at[:, 0, :].rearrange("p (h d) -> p h d", d=DK), vcls[:, :, 0:DK]).then_inc(vcls_ready, 1)
            dve.wait_ge(wq_hi_ready, 1)
            V.tensor_tensor(wq_lo[:, :, :], wq_in[:, :, :], wq_hi[:, :, :].bitcast(F32), ALU.subtract)
            dve.wait_ge(wv_hi_ready, 1)
            V.tensor_tensor(wv_lo[:, :, :], wv_in[:, :, :], wv_hi[:, :, :].bitcast(F32), ALU.subtract).then_inc(attn_split, 1)
            for t in range(NT):
                take_x("pro", 0, t, 0)
                take_x("pro", 0, t, 1)
                if t:
                    take_h("pro", 0, t - 1)
            take_h("pro", 0, NT - 1)
            layer_norm(1, hn, NT)
            take_z("pro", 0)
            for c in range(NC - 1):
                w2_rest(c)
            tail("pro", 0, 0, True, 1)
            before = step.n
            turn("body", 0, 1)
            per = step.n - before
            with dve.Fori(1, B - 1) as b:
                step.loop(b - 1, per)
                turn("body", b, NT)
            step.end(B - 2, per)
            turn("last", B - 1, NT, False)
            for f in range(NF):
                g_rest(B, f, S)
            finish(B, NT)

        @block.tensor
        def _(pe):
            T = nc.tensor

            def d_bank(part, name, b):
                ps, full, free, k = d_at(part, name, b)
                wait(pe, free, k)
                return ps, full

            def s_bank(n, b):
                ps, full, free, k = s_at(n, b)
                wait(pe, free, k)
                return ps, full

            def transpose_tiles(part, name, b, src, tiles):
                for ht in range(HT):
                    ps, full = d_bank(part, (name, ht), b)
                    for t in range(tiles):
                        ins = T.transpose(ps[:, t * P:(t + 1) * P], src[:, t, ht * P:(ht + 1) * P], ident[:, :])
                    ins.then_inc(full, 1)

            def attention_half(part, b, ht):
                pe.wait_ge(at_ready, 4 * b + 2 * ht + 2)
                ps, full = d_bank(part, ("att", ht), b)
                for t in range(NT):
                    ins = T.transpose(ps[:, t * P:(t + 1) * P], at[:, t, ht * P:(ht + 1) * P], ident[:, :])
                ins.then_inc(full, 1)

            def wo_half(part, b, k, between):
                taken(pe, part, ("att", k), b)
                for t in range(NT):
                    if t % 2 == 0:
                        if k == 0:
                            ps, full = d_bank(part, ("wo", t), b)
                        else:
                            ps, full, _, _ = d_at(part, ("wo", t), b)
                    ins = T.matmul(ps[:, D * (t % 2):D * (t % 2 + 1)], aT[k][:, t * P:(t + 1) * P], wo[:, k, :],
                                   start=(k == 0 and t % 2 == 0), stop=(k == HT - 1), skip_group_check=True)
                    if t % 2 == 1 and k == HT - 1:
                        ins.then_inc(full, 1)
                    between()

            def xt(part, b, t, half):
                nb = 0 if part == "pro" else b + 1
                if half == 0:
                    pe.wait_ge(x_full[t % 2], 32 * nb + 16 * (t // 2) + 16)
                ps, full = d_bank(part, ("xt", t, half), b)
                for k in range(4):
                    ins = T.transpose(ps[:, k * P:(k + 1) * P], xin[:, t % 2, (4 * half + k) * P:(4 * half + k + 1) * P], ident[:, :])
                ins.then_inc(full, 1)

            def tok(part, b, t, quarter):
                if quarter % 2 == 0:
                    taken(pe, part, ("xt", t, quarter // 2), b)
                if quarter == 0:
                    ps, full = d_bank(part, ("tok", t), b)
                else:
                    ps, full, _, _ = d_at(part, ("tok", t), b)
                for k in (2 * quarter, 2 * quarter + 1):
                    for p, (xs, w) in enumerate(((xT_hi, wtok_hi), (xT_hi, wtok_lo), (xT_lo, wtok_hi))):
                        ins = T.matmul(ps[:, 0:D], xs[:, 2 * (t % 2) + k // 4, (k % 4) * P:(k % 4 + 1) * P], w[:, k, :],
                                       start=(k == 0 and p == 0), stop=(k == KX - 1 and p == 2), skip_group_check=True)
                if quarter == 3:
                    ins.then_inc(full, 1)

            def project(part, name, b, lhs, rhs, width):
                ps, full = d_bank(part, name, b)
                for k in range(HT):
                    ins = T.matmul(ps[:, 0:width], lhs(k), rhs(k), start=(k == 0), stop=(k == HT - 1))
                ins.then_inc(full, 1)

            def bring_up(part, b):
                def zt1(ht):
                    ps, full = d_bank(part, ("zt1", ht), b)
                    for t in range(NT):
                        ins = T.transpose(ps[:, t * P:(t + 1) * P], z[:, t, ht * P:(ht + 1) * P], ident[:, :])
                    ins.then_inc(full, 1)

                def qk0():
                    both(part, "zt1", b)
                    qk_tile(part, b, 0)

                def after_norm():
                    pe.wait_ge(z_ready, 2 if part == "pro" else 2 * b + 4)
                    zt1(0)

                return [after_norm, lambda: zt1(1), qk0]

            def nothing():
                pass

            def qk_tile(part, b, j, between=lambda: None):
                if part == "pro" and j == 0:
                    pe.wait_ge(attn_split, 1)
                ps, full = d_bank(part, ("qk", j), b)
                for k in range(HT):
                    for p, (w, zs) in enumerate(((wq_hi, zT_hi), (wq_hi, zT_lo), (wq_lo, zT_hi))):
                        ins = T.matmul(ps[:, :], w[:, k, j * P:(j + 1) * P], zs[:, k, :], start=(k == 0 and p == 0),
                                       stop=(k == HT - 1 and p == 2), skip_group_check=True)
                        if (k, p) != (HT - 1, 2):
                            between()
                ins.then_inc(full, 1)

            def back(part, b, q):
                pe.wait_ge(ot_ready, 4 * b + q + 1)
                ps, full = d_bank(part, ("bt", q), b)
                for t in range(NT):
                    ins = T.transpose(ps[:, t * P:(t + 1) * P], ot[:, q % 2, t * P:(t + 1) * P], ident[:, :])
                ins.then_inc(full, 1)

            def both(part, name, b):
                taken(pe, part, (name, 0), b)
                taken(pe, part, (name, 1), b)

            def pair(part, name, b, t0, tiles, products):
                ps, full = d_bank(part, (name, t0), b)
                for t in range(t0, min(t0 + 2, tiles)):
                    for k in range(HT):
                        for p, (src, w) in enumerate(products):
                            ins = T.matmul(ps[:, D * (t - t0):D * (t - t0 + 1)], src[:, k, t * P:(t + 1) * P], w[:, k, :],
                                           start=(k == 0 and p == 0), stop=(k == HT - 1 and p == len(products) - 1), skip_group_check=True)
                ins.then_inc(full, 1)

            def w1_tile(part, b, t):
                ps, full = d_bank(part, ("w1", t), b)
                for k in range(HT):
                    ins = T.matmul(ps[:, :], aT[k][:, t * P:(t + 1) * P], w1_sb[:, k, :], start=(k == 0), stop=(k == HT - 1))
                ins.then_inc(full, 1)

            def weighted(part, b, t):
                taken(pe, part, ("w1", t), b)
                ps, full = d_bank(part, ("tt", t), b)
                for c in range(NC):
                    ins = T.transpose(ps[:, c * P:(c + 1) * P], tm[:, t % 2, c * P:(c + 1) * P], ident[:, :])
                ins.then_inc(full, 1)

            def tail(part, b, new, tiles):
                scores = cls_scores(0 if part == "pro" else b + 1, part, b) if new else iter(())

                def one_score():
                    next(scores, None)

                if part == "pro":
                    qk_tile(part, b, 1)
                    qk_tile(part, b, 2)
                    pe.wait_ge(vcls_ready, 2)
                    transpose_tiles(part, "att", b, at, 1)
                    qk_tile(part, b, 3)
                    both(part, "att", b)
                    project(part, ("wo", 0), b, lambda k: aT[k][:, 0:P], lambda k: wo[:, k, :], D)
                else:
                    values(b, CHUNKS - 1)
                    if new:
                        qk_tile(part, b, 1)
                    back(part, b, 3)
                    wo_half(part, b, 0, nothing)
                    attention_half(part, b, 1)
                    if new:
                        qk_tile(part, b, 2)
                    wo_half(part, b, 1, one_score)
                    if new:
                        qk_tile(part, b, 3, one_score)
                for _ in scores:
                    pass
                if new:
                    for t in (0, 2):
                        pair(part, "v", b, t, NT, [(zT_hi, wv_hi), (zT_hi, wv_lo), (zT_lo, wv_hi)])
                pe.wait_ge(z_ready, 2 * b + 5 if part == "body" else {"pro": 3, "last": 2 * B + 2}[part])
                if tiles == NT:
                    pe.wait_ge(z_late_ready, b + 1)
                transpose_tiles(part, "zt2", b, z, tiles)
                both(part, "zt2", b)
                if part == "pro":
                    pe.wait_ge(ffn_in, 64)
                ps, full = d_bank(part, ("lt",), b)
                for k in range(HT):
                    ins = T.matmul(ps[0:NE, 0:tiles * P], rw_sb[:, k, :], aT[k][:, 0:tiles * P], start=(k == 0), stop=(k == HT - 1))
                ins.then_inc(full, 1)
                w1_tile(part, b, 0)
                taken(pe, part, ("lt",), b)
                ps, full = d_bank(part, ("rt",), b)
                for t in range(tiles):
                    ins = T.transpose(ps[:, t * P:(t + 1) * P], lgT[:, t * P:(t + 1) * P], ident[:, :])
                ins.then_inc(full, 1)
                for t in range(1, tiles - 1):
                    w1_tile(part, b, t)
                weighted(part, b, 0)
                if tiles == NT:
                    w1_tile(part, b, NT - 1)
                for t in range(1, tiles):
                    weighted(part, b, t)

            def ffn_mid(part, b, f, n, between=lambda: None):
                if f == 0 and first(b):
                    pe.wait_ge(ffn_split, 1)
                ps, full = d_bank(part, ("w2", f), b)
                width = n // 2 if f == 0 and n == S else n
                for t0 in range(0, n, width):
                    if f == 0:
                        for t in range(t0 // P, (t0 + width) // P):
                            taken(pe, tail_of(b)[0], ("tt", t), tail_of(b)[1])
                    for c in range(NC):
                        for p, (w, act) in enumerate(((w2_hi, tT_hi), (w2_hi, tT_lo), (w2_lo, tT_hi))):
                            ins = T.matmul(ps[:, t0:t0 + width], w[:, c, f * P:(f + 1) * P], act[:, c, t0:t0 + width],
                                           start=(c == 0 and p == 0), stop=(c == NC - 1 and p == 2), skip_group_check=True)
                        if c < NC - 1:
                            between()
                ins.then_inc(full, 1)
                between()

            def ffn_out(part, b, f, n, between=lambda: None):
                pe.wait_ge(g_lo_ready, NF * b + f + 1)
                if f == 0:
                    wait(pe, ot_ready, 4 * b)
                for t in range(n // P):
                    for p, (act, w) in enumerate(((g_hi, lw_hi), (g_hi, lw_lo), (g_lo, lw_hi))):
                        ins = T.matmul(bank[3 + t // 2][:, D * (t % 2):D * (t % 2 + 1)], act[:, f % 2, t * P:(t + 1) * P], w[:, f, :],
                                       start=(f == 0 and t % 2 == 0 and p == 0), stop=(f == NF - 1 and p == 2), skip_group_check=True)
                    if t < n // P - 1:
                        between()
                ins.then_inc(g_used if f < NF - 1 else lin_full, 1)
                for t in range(n // P - 1, NT):
                    between()

            def cls_scores(nb, part, b):
                taken(pe, part, ("qk", 1), b)
                if first(nb):
                    pe.wait_ge(kblk_ready, 1)
                ps, full = s_bank(S_CLS, nb)
                for qt in range(NT):
                    for ht in range(HT):
                        ins = T.matmul(ps[:, qt * NH:(qt + 1) * NH], qT[:, ht, qt * P:(qt + 1) * P], kblk[:, ht, :],
                                       start=(ht == 0), stop=(ht == HT - 1), skip_group_check=True)
                        if (qt, ht) == (NT - 1, HT - 1):
                            ins.then_inc(full, 1)
                        yield

            def max_unit(b, i):
                qt, h0, w = MAX_UNITS[i]
                n = P * (qt + 1)
                ps, full = s_bank(S_MAX + i, b)
                if i == 0:
                    pe.wait_ge(scr_r, 2 * len(Q_PART) * 16 * (b + 1))
                for j in range(w):
                    T.matmul(ps[:, j * n:(j + 1) * n], qs[0:STACK, h0 + j, qt * P:(qt + 1) * P], ks[0:STACK, h0 + j, 0:n],
                             start=True, stop=False, skip_group_check=True)
                    ins = T.matmul(ps[:, (j + 1) * n - P:(j + 1) * n], identb[:, :], maskq[:, :],
                                   start=False, stop=True, skip_group_check=True)
                ins.then_inc(full, 1)

            def turn_maxima(b):
                pe.wait_ge(mhl_ready, b + 1)
                ps, full = s_bank(S_MT, b)
                for t in range(NT):
                    ins = T.matmul(ps[STACK:P, t * P:(t + 1) * P], mhl[:, t, :], identb[:, :], start=True, stop=True)
                ins.then_inc(full, 1)

            def exp_unit(b, c, u, j, w):
                kt, n = c % NT, S - P * (c % NT)
                ps, full = s_bank(u, b)
                for i in range(w):
                    h = 4 * (c // NT) + j + i
                    T.matmul(ps[:, i * n:(i + 1) * n], ks[:, h, kt * P:(kt + 1) * P], qs[:, h, kt * P:S],
                             start=True, stop=False, skip_group_check=True)
                    ins = T.matmul(ps[:, i * n:i * n + P], identb[:, :], maskk[:, :], start=False, stop=True, skip_group_check=True)
                ins.then_inc(full, 1)

            def values(b, c):
                q, kt = c // NT, c % NT
                n = S - P * kt
                for u, _, _ in units_of(c):
                    score_taken(pe, u, b)
                if kt == 0:
                    if q < 2:
                        pe.wait_ge(out_ready, 4 * b + 1)
                    else:
                        pe.wait_ge(ot_ready, 4 * b + q - 1)
                for j in range(4):
                    ins = T.matmul(bank[3 + q % 2][32 * j:32 * j + 32, P * kt:S], va[:, kt, 4 * q + j, :], pt[:, c % 2, j, 0:n],
                                   start=(kt == 0), stop=(kt == NT - 1), skip_group_check=True)
                ins.then_inc(pv_full if kt == NT - 1 else pv_used, 1)

            def attend_group(part, b, q, new):
                c = NT * q
                if first(b) and q == 0:
                    pe.wait_ge(stack_set, 1)
                pe.wait_ge(qs_max, 4 * b + q + 1)
                units = [[lambda c=c, u=u: exp_unit(b, c, *u) for u in units_of(c)] for c in range(c, c + NT)]
                tok_step = [lambda i=i: tok(part, b, q + 1, i) for i in range(4)] if new and q + 1 < NT else [nothing] * 4
                back_step = (lambda: back(part, b, q - 1)) if q else nothing
                before = (lambda: values(b, c - 1)) if q else nothing
                x_step = [lambda i=i: xt(part, b, q + 2, i) for i in range(2)] if new and q + 2 < NT else [nothing] * 2
                first_half = (lambda: attention_half(part, b, 0)) if q + 1 == 4 else nothing
                up = bring_up(part, b) if new and q + 1 == NT else [nothing] * 3
                for item in (
                        units[0][0], tok_step[0], units[0][1], before, units[0][2], tok_step[1], up[0], units[0][3], tok_step[2], up[1],
                        units[1][0], units[1][1], lambda: values(b, c), tok_step[3], units[1][2], back_step,
                        units[1][3], x_step[0], units[2][0], units[2][1], lambda: values(b, c + 1), up[2],
                        units[3][0], x_step[1], first_half, lambda: values(b, c + 2)):
                    item()

            def turn(part, b, n, new=True):
                units = iter(range(len(MAX_UNITS)))
                def one_unit():
                    for i in units:
                        max_unit(b, i)
                        break

                for f in range(NF - 1):
                    between = one_unit if f >= MAX_FROM else nothing
                    ffn_mid(part, b, f, n, between)
                    if f:
                        ffn_out(part, b, f - 1, n, between)
                for i in units:
                    max_unit(b, i)
                if new:
                    xt(part, b, 0, 0)
                    xt(part, b, 0, 1)
                ffn_mid(part, b, NF - 1, n)
                turn_maxima(b)
                ffn_out(part, b, NF - 2, n)
                if new:
                    xt(part, b, 1, 0)
                    xt(part, b, 1, 1)
                ffn_out(part, b, NF - 1, n)
                if new:
                    for i in range(4):
                        tok(part, b, 0, i)
                for q in range(4):
                    attend_group(part, b, q, new)
                tail(part, b, new, NT)

            pe.wait_ge(consts, IDENT_CONSTS)
            pe.wait_ge(tok_w, 32)
            for i in range(HT):
                ps, full = d_bank("pro", ("ws", i), 0)
                for a in range(HT):
                    ins = T.transpose(ps[:, a * P:(a + 1) * P], ws_sb[:, a, i * P:(i + 1) * P], ident[:, :])
                ins.then_inc(full, 1)
            ps, full = d_bank("pro", ("wt",), 0)
            for a in range(HT):
                ins = T.transpose(ps[0:DD, a * P:(a + 1) * P], w_sb[:, a, :], ident[:, :])
            ins.then_inc(full, 1)
            pe.wait_ge(consts, SPREAD_CONSTS)
            taken(pe, "pro", ("wt",), 0)
            ps, full = d_bank("pro", ("wrep",), 0)
            T.matmul(ps[:, 0:D], spread4[:, :], wT[:, :], start=True, stop=True).then_inc(full, 1)
            both("pro", "ws", 0)
            for k in range(KX):
                ps, full = d_bank("pro", ("wtok", k), 0)
                T.matmul(ps[:, 0:D], spread[:, k % 4, :], wsT[:, k // 4, :], start=True, stop=True).then_inc(full, 1)
            pe.wait_ge(z_ready, 1)
            transpose_tiles("pro", "czt", 0, x1, 1)
            both("pro", "czt", 0)
            pe.wait_ge(attn_w, 64)
            ps, full = d_bank("pro", ("ck",), 0)
            for ht in range(HT):
                for k in range(HT):
                    ins = T.matmul(ps[:, ht * P:(ht + 1) * P], wq_in[:, k, D + ht * P:D + (ht + 1) * P], aT[k][:, 0:P],
                                   start=(k == 0), stop=(k == HT - 1))
            ins.then_inc(full, 1)
            project("pro", ("cv",), 0, lambda k: aT[k][:, 0:P], lambda k: wv_in[:, k, :], D)
            for i in range(KX):
                taken(pe, "pro", ("wtok", i), 0)
            for t in range(NT):
                for half in range(2):
                    xt("pro", 0, t, half)
                if t:
                    for i in range(4):
                        tok("pro", 0, t - 1, i)
            for i in range(4):
                tok("pro", 0, NT - 1, i)
            for stage in bring_up("pro", 0):
                stage()
            tail("pro", 0, True, 1)
            pe.wait_ge(consts, CONSTS)
            pe.wait_ge(identb_ready, 1)
            turn("body", 0, P)
            with pe.Fori(1, B - 1) as b:
                turn("body", b, S)
            turn("last", B - 1, S, False)
            for f in range(NF):
                ffn_mid("end", B, f, S)
                if f:
                    ffn_out("end", B, f - 1, S)
            ffn_out("end", B, NF - 1, S)


INPUTS = ["x", "cls_tok", "L0_tok_weight", "L0_tok_weighted_sum", "L0_attn_WQ", "L0_attn_WK", "L0_attn_WV", "L0_attn_WO",
          "L0_ffn_router_w", "L0_ffn_router_b", "L0_ffn_w1", "L0_ffn_w2", "L0_ffn_lin2_w", "L0_ffn_lin2_b"]


def kernel(**inputs):
    import numpy as np
    import concourse.bacc as bacc
    from concourse.bass_utils import run_bass_kernel_spmd

    nc = bacc.Bacc("TRN2", target_bir_lowering=False, num_devices=1)
    arrays, args = {}, []
    for name in INPUTS:
        a = np.ascontiguousarray(inputs[name])
        if name == "x":
            a = a.reshape(B, S, IN * DD)
        arrays["in_" + name] = a
        args.append(nc.dram_tensor("in_" + name, a.shape, mybir.dt.from_np(a.dtype), kind="ExternalInput").ap())
    args.append(nc.dram_tensor("out_h", (B, S + 1, D), F32, kind="ExternalOutput").ap())
    build(nc, *args)
    r = run_bass_kernel_spmd(nc, [arrays], core_ids=[0])
    return r.results[0]["out_h"]
```
